# Optimizing a Trainium2 kernel written in Bass

```python
import numpy as np
import jax
import jax.numpy as jnp

def _softmax(x, axis=-1):
    return jax.nn.softmax(x, axis=axis)

def _gelu(x):
    return jax.nn.gelu(x, approximate=True)

def _silu(x):
    return jax.nn.silu(x)

def _sigmoid(x):
    return jax.nn.sigmoid(x)

def _layernorm(x, axis=-1, eps=1e-05):
    m = jnp.mean(x, axis=axis, keepdims=True)
    v = jnp.var(x, axis=axis, keepdims=True)
    return (x - m) / jnp.sqrt(v + eps)

def _scatter_add(tgt, idx, src, axis=0):
    return tgt.at[idx].add(src)

def _segment_sum(src, seg, n):
    return jax.ops.segment_sum(src, seg, n)
kernel_name = 'mk_macaron_d1_jaxref_r8_ad4abf'

def setup_inputs(seed: int=0):
    np.random.seed(seed)
    _w = jnp.asarray

    def _L0_attn_setup():
        import jax, jax.numpy as jnp
        import numpy as np
        B, N, D = (4, 512, 128)
        EPS = 1e-05
        key = jax.random.key(seed)
        kx, kq, kk, kv, ka, kg, ko = jax.random.split(key, 7)
        s = D ** (-0.5)
        return {'x': jax.random.normal(kx, (B, N, D), dtype=jnp.float32), 'gamma': jnp.ones((D,), dtype=jnp.float32), 'wq': jax.random.normal(kq, (D, D), dtype=jnp.float32) * s, 'wk': jax.random.normal(kk, (D, D), dtype=jnp.float32) * s, 'wv': jax.random.normal(kv, (D, D), dtype=jnp.float32) * s, 'wa': jax.random.normal(ka, (D, 2 * D), dtype=jnp.float32) * s, 'wg': jax.random.normal(kg, (D, D), dtype=jnp.float32) * s, 'wo': jax.random.normal(ko, (D, D), dtype=jnp.float32) * s}
    _L0_attn_in = _L0_attn_setup()

    def _L0_ffn_setup():
        import jax, jax.numpy as jnp
        import numpy as np
        B, S, D, E, H = (2, 128, 128, 16, 256)
        TOP_K = 2
        TEMP = 1.0
        key = jax.random.key(seed)
        ks = jax.random.split(key, 4)
        sc_d = 1.0 / np.sqrt(D)
        sc_h = 1.0 / np.sqrt(H)
        return {'x': jax.random.normal(ks[0], (B, S, D), dtype=jnp.float32), 'Wr': jax.random.normal(ks[1], (D, E), dtype=jnp.float32) * sc_d, 'br': jnp.zeros((E,), dtype=jnp.float32), 'W1': jax.random.normal(ks[2], (E, D, H), dtype=jnp.float32) * sc_d, 'b1': jnp.zeros((E, H), dtype=jnp.float32), 'W2': jax.random.normal(ks[3], (E, H, D), dtype=jnp.float32) * sc_h, 'b2': jnp.zeros((E, D), dtype=jnp.float32)}
    _L0_ffn_in = _L0_ffn_setup()
    _d = {'L0_attn_x': _L0_attn_in['x'], 'L0_attn_gamma': _L0_attn_in['gamma'], 'L0_attn_wq': _L0_attn_in['wq'], 'L0_attn_wk': _L0_attn_in['wk'], 'L0_attn_wv': _L0_attn_in['wv'], 'L0_attn_wa': _L0_attn_in['wa'], 'L0_attn_wg': _L0_attn_in['wg'], 'L0_attn_wo': _L0_attn_in['wo'], 'L0_ffn_Wr': _L0_ffn_in['Wr'], 'L0_ffn_br': _L0_ffn_in['br'], 'L0_ffn_W1': _L0_ffn_in['W1'], 'L0_ffn_b1': _L0_ffn_in['b1'], 'L0_ffn_W2': _L0_ffn_in['W2'], 'L0_ffn_b2': _L0_ffn_in['b2']}
    _x0 = _d['L0_attn_x']
    _d['L0_attn_x'] = jax.random.normal(jax.random.fold_in(jax.random.key(seed), 1), (32, 256, 128), dtype=_x0.dtype)
    del _x0
    return _d

def reference(L0_attn_x, L0_attn_gamma, L0_attn_wq, L0_attn_wk, L0_attn_wv, L0_attn_wa, L0_attn_wg, L0_attn_wo, L0_ffn_Wr, L0_ffn_br, L0_ffn_W1, L0_ffn_b1, L0_ffn_W2, L0_ffn_b2):

    def _L0_attn_ref(x, gamma, wq, wk, wv, wa, wg, wo):
        import jax, jax.numpy as jnp
        import numpy as np
        B, N, D = (4, 512, 128)
        EPS = 1e-05
        dim = x.shape[-1]
        inv_norm = jax.lax.rsqrt(jnp.sum(jnp.square(x), axis=-1, keepdims=True) + EPS)
        xn = inv_norm * x * gamma * dim ** 0.5
        q = xn @ wq
        k = xn @ wk
        v = xn @ wv
        a = xn @ wa
        g = xn @ wg
        a_real, a_imag = jnp.split(a, 2, axis=-1)
        a_complex = jax.lax.complex(a_real, a_imag)
        magnitude = jax.nn.sigmoid(jnp.abs(a_complex))
        phase = jnp.angle(a_complex)
        a_complex = jax.lax.complex(magnitude * jnp.cos(phase), magnitude * jnp.sin(phase))
        kv_ = (k * v).astype(a_complex.dtype)

        def binary_operator(e_i, e_j):
            a_i, kv_i = e_i
            a_j, kv_j = e_j
            return (a_j * a_i, a_j * kv_i + kv_j)
        _, y = jax.lax.associative_scan(binary_operator, (a_complex, kv_), axis=1)
        y = q * jnp.real(y)
        y = y * jax.nn.silu(g)
        return y @ wo

    def _L0_ffn_ref(x, Wr, br, W1, b1, W2, b2):
        import jax, jax.numpy as jnp
        import numpy as np
        B, S, D, E, H = (2, 128, 128, 16, 256)
        TOP_K = 2
        TEMP = 1.0
        token_shape = x.shape[:-1]
        d = x.shape[-1]
        xt = x.reshape(-1, d)
        T = xt.shape[0]
        logits = (xt @ Wr + br) / TEMP
        probs = jax.nn.softmax(logits, axis=-1)
        w, idx = jax.lax.top_k(probs, TOP_K)
        w = w / jnp.clip(jnp.sum(w, axis=-1, keepdims=True), 1e-09)
        comb = jnp.zeros((T, E), dtype=xt.dtype)
        comb = comb.at[jnp.arange(T)[:, None], idx].add(w)
        h = jax.nn.gelu(jnp.einsum('td,edh->teh', xt, W1) + b1, approximate=False)
        o = jnp.einsum('teh,eho->teo', h, W2) + b2
        y = jnp.einsum('teo,te->to', o, comb)
        y = xt + y
        return y.reshape(*token_shape, d)
    x = L0_attn_x
    x = x + 0.5 * _L0_ffn_ref(_layernorm(x, axis=-1), L0_ffn_Wr, L0_ffn_br, L0_ffn_W1, L0_ffn_b1, L0_ffn_W2, L0_ffn_b2)
    x = x + _L0_attn_ref(_layernorm(x, axis=-1), L0_attn_gamma, L0_attn_wq, L0_attn_wk, L0_attn_wv, L0_attn_wa, L0_attn_wg, L0_attn_wo)
    x = x + 0.5 * _L0_ffn_ref(_layernorm(x, axis=-1), L0_ffn_Wr, L0_ffn_br, L0_ffn_W1, L0_ffn_b1, L0_ffn_W2, L0_ffn_b2)
    return x

_drawn_inputs = setup_inputs


def setup_inputs(seed=0):
    import zlib

    import numpy as np

    out = dict(_drawn_inputs(seed))
    spreads = {'L0_attn_gamma': (1.0, 0.2),
     'L0_ffn_br': (0.0, 0.1),
     'L0_ffn_b1': (0.0, 0.1),
     'L0_ffn_b2': (0.0, 0.1)}
    factors = {}
    for name, (base, spread) in spreads.items():
        noise = np.random.default_rng([zlib.crc32(name.encode()), seed]).standard_normal(out[name].shape)
        drawn = base * np.exp(spread * noise) if base else spread * noise
        out[name] = jnp.asarray(drawn.astype(out[name].dtype))
    for name, factor in factors.items():
        out[name] = (out[name] * factor).astype(out[name].dtype)
    return out
```

```python
import concourse.bass as bass
from concourse import mybir
from contextlib import ExitStack

P = 128
D = 128
B, N = 32, 256
E, H = 16, 256
G = 4
T = B * N // G // P
C = N // T
BG = B // G
NT = 2 * T + E
NP = NT // 2
SLOTS = 4
EPS = 1e-5
TINY = 1e-18

ORDER = [("R", 0, 0), ("R", 0, 1), ("E", 0, 0), ("R", 0, 2), ("C", 0, 0), ("A", 0), ("E", 0, 1), ("A2", 0),
         ("A3", 0), ("R", 1, 0), ("R", 0, 3), ("C", 0, 1), ("A", 1), ("E", 1, 0), ("A2", 1), ("A3", 1), ("R", 1, 1),
         ("E", 0, 2), ("C", 1, 0), ("C", 0, 2), ("A", 2), ("E", 1, 1), ("A2", 2), ("A3", 2), ("R", 1, 2),
         ("E", 0, 3), ("C", 1, 1), ("C", 0, 3), ("A", 3), ("E", 1, 2), ("A2", 3), ("A3", 3), ("R", 1, 3),
         ("C", 1, 2), ("E", 1, 3), ("C", 1, 3)]


def build(nc, x, gamma, wq, wk, wv, wa, wg, wo, wr, br, w1, b1, w2, b2, out):
    f32, bf16, i32, u32 = mybir.dt.float32, mybir.dt.bfloat16, mybir.dt.int32, mybir.dt.uint32
    ALU = mybir.AluOpType
    ACT = mybir.ActivationFunctionType
    AX = mybir.AxisListType
    ds = bass.ds
    add, sub, mult = ALU.add, ALU.subtract, ALU.mult

    x_v = x.rearrange("(g b) (c l) d -> g (b c) l d", g=G, l=T)
    out_v = out.rearrange("(g b) (c l) d -> g (b c) l d", g=G, l=T)
    rows_in = [nc.dram_tensor(f"rows_in{g}", (NT * P, D), f32, kind="Internal").ap() for g in range(G)]
    rows_out = [nc.dram_tensor(f"rows_out{g}", (NT * P, D), f32, kind="Internal").ap() for g in range(G)]
    bias1_parts = nc.dram_tensor("bias1_parts", (3, E, H), bf16, kind="Internal").ap()
    bias2_parts = nc.dram_tensor("bias2_parts", (3, E, D), bf16, kind="Internal").ap()

    kind_no = {}
    psum_before = {}
    seen, last = {}, None
    for st in ORDER:
        kind_no[st] = seen.get(st[0], 0)
        seen[st[0]] = kind_no[st] + 1
        psum_before[st] = last
        if st[0] in ("R", "E", "A", "A3"):
            last = st

    with ExitStack() as ctx:
        def sb(name, shape, dt):
            return ctx.enter_context(nc.sbuf_tensor(name, shape, dt))

        def sem(name):
            return ctx.enter_context(nc.semaphore(name))

        X = sb("X", [P, G, T, D], f32)
        XL = sb("XL", [P, 2, T, D], f32)
        W1 = sb("W1", [P, E * H], f32)
        W2 = sb("W2", [P, E * H], f32)
        B1R = sb("B1R", [3, E * H], bf16)
        B2R = sb("B2R", [3, E * D], bf16)
        WA = sb("WA", [P, 6, D], f32)
        WO = sb("WO", [P, D], f32)
        WR = sb("WR", [P, E], f32)
        BR = sb("BR", [P, E], f32)
        GM = sb("GM", [P, 1], f32)
        GS = sb("GS", [P, 1], f32)
        ident = sb("ident", [P, P], f32)
        onesf = sb("onesf", [P, P], f32)
        before = sb("before", [P, P], bf16)
        ones = sb("ones", [P, P], bf16)
        iota_i = sb("iota_i", [P, NT], i32)
        iota_f = sb("iota_f", [P, NT], f32)
        keep = sb("keep", [P, E, T + 1], f32)
        IDX = sb("IDX", [P, G, T, 2], u32)
        WGT = sb("WGT", [P, G, 2, T], f32)
        TE = sb("TE", [1, G, NT], i32)
        stats = sb("stats", [P, T, 6], f32)
        m2 = sb("m2", [P, T], f32)
        df = sb("df", [P, T], f32)
        var = sb("var", [P, T], f32)
        vh = sb("vh", [P, T], f32)
        seed = sb("seed", [P, T], u32)
        rs = sb("rs", [P, T], f32)
        na = sb("na", [P, T], f32)
        nb = sb("nb", [P, T], f32)
        XT = sb("XT", [P, T * D], f32)
        LG = sb("LG", [P, T, E], f32)
        MX = sb("MX", [P, T, 8], f32)
        IX = sb("IX", [P, T, 8], u32)
        IXF = sb("IXF", [P, T, 2], f32)
        gap = sb("gap", [P, T], f32)
        gexp = sb("gexp", [P, T], f32)
        den = sb("den", [P, T], f32)
        mask = sb("mask", [P, T, E], bf16)
        cnt = sb("cnt", [P, E, T + 1], f32)
        off = sb("off", [P, E, T + 1], f32)
        nte = sb("nte", [P, E], f32)
        cum = sb("cum", [P, E], f32)
        basee = sb("basee", [P, E], f32)
        pos = sb("pos", [P, T, E], f32)
        rowf = sb("rowf", [P, T, 2], f32)
        tef = sb("tef", [1, NT], f32)
        xs = sb("xs", [P, SLOTS, 2, D], f32)
        xsT = sb("xsT", [P, 2, 2 * P], f32)
        hid = sb("hid", [P, 2, 2 * H], f32)
        hidT = sb("hidT", [P, 2, 4 * P], f32)
        eo = sb("eo", [P, SLOTS, 2, D], f32)
        got = sb("got", [P, SLOTS, 2, D], f32)
        kv = sb("kv", [P, T * P], f32)
        cr = sb("cr", [P, T, P], f32)
        ci = sb("ci", [P, T, P], f32)
        qg = sb("qg", [P, T * P], f32)
        S = sb("S", [P, T, 4, P], f32)
        scratch = sb("scratch", [P, 1024], f32)
        K = sb("K", [P, 2, BG, C], f32)
        k1 = sb("k1", [P, 2, BG], f32)
        k2 = sb("k2", [P, 2, BG], f32)
        S_flat = S[:].rearrange("p l f c -> p (l f c)")
        W = T * P
        tmp = [S_flat[:, i * W:(i + 1) * W] for i in range(4)]
        XN = kv[:].rearrange("p (l d) -> p l d", l=T)
        zeros = kv[:]
        b1f, b2f = S_flat[0:E, 0:H], S_flat[0:E, H:H + D]
        b1r, b2r = S_flat[0:E, 512:512 + H], S_flat[0:E, 512 + H:512 + H + D]
        b1p = S_flat[0:E, 1024:2048].bitcast(bf16)[:, 0:3 * H].rearrange("e (k h) -> e k h", k=3)
        b2p = S_flat[0:E, 2048:3072].bitcast(bf16)[:, 0:3 * D].rearrange("e (k h) -> e k h", k=3)
        hot = scratch[:, 0:512].rearrange("p (k t e) -> p k t e", k=2, t=T)
        sel = scratch[:, 512:1024].rearrange("p (k t e) -> p k t e", k=2, t=T)
        tcmp = scratch[0:1, 0:NT * E].rearrange("p (t e) -> p t e", t=NT)
        t1 = scratch[:, 0:512].rearrange("p (a r c) -> p a r c", a=2, r=2)
        t2 = scratch[:, 512:1024].rearrange("p (a r c) -> p a r c", a=2, r=2)
        ps = [ctx.enter_context(nc.psum_tensor(f"bank{i}", [P, 512], f32)) for i in range(8)]

        x_in = [sem(f"x_in{g}") for g in range(G)]
        zeroed = [sem(f"zeroed{g}") for g in range(G)]
        w_in, ew_in, bias_in, parts_out, bias_rows = sem("w_in"), sem("ew_in"), sem("bias_in"), sem("parts_out"), sem("bias_rows")
        consts, zero_ready, parts_ready = sem("consts"), sem("zero_ready"), sem("parts_ready")
        dve_chain, pool_chain = sem("dve_chain"), sem("pool_chain")
        rank_read, x_added, gs_ready = sem("rank_read"), sem("x_added"), sem("gs_ready")
        xl_ready, xt_ps, xt_sb, logits_ps = sem("xl_ready"), sem("xt_ps"), sem("xt_sb"), sem("logits_ps")
        gap_ready, gap_exp, mask_ready, rank_ps, rows_ready = (sem("gap_ready"), sem("gap_exp"), sem("mask_ready"),
                                                             sem("rank_ps"), sem("rows_ready"))
        scattered = [sem(f"scattered{i}") for i in range(2)]
        xs_in = [sem(f"xs_in{i}") for i in range(SLOTS)]
        eo_out = [sem(f"eo_out{i}") for i in range(SLOTS)]
        xsT_ps, xsT_sb, hid_ps, hid_sb = sem("xsT_ps"), sem("xsT_sb"), sem("hid_ps"), sem("hid_sb")
        hidT_ps, hidT_sb, eo_ps, eo_sb = sem("hidT_ps"), sem("hidT_sb"), sem("eo_ps"), sem("eo_sb")
        got_in = [sem(f"got_in{i}") for i in range(SLOTS)]
        combined = sem("combined")
        xn_ready, xnT_ps, xnT_sb = sem("xn_ready"), sem("xnT_ps"), sem("xnT_sb")
        proj_ps, proj_act, proj_dve = sem("proj_ps"), sem("proj_act"), sem("proj_dve")
        r2_ready, r_ready, m_ready, sg_ready = sem("r2_ready"), sem("r_ready"), sem("m_ready"), sem("sg_ready")
        y_ready, wo_ps, stored = sem("y_ready"), sem("wo_ps"), sem("stored")

        block = ctx.enter_context(nc.Block())
        small_weights, expert_weights = 9 * 16, 3 * 16

        @block.sync
        def _(sp):
            sp.dma_start(X[:, 0, :, :], x_v[0]).then_inc(x_in[0], 16)
            sp.dma_start(b1f, b1).then_inc(bias_in, 16)
            sp.dma_start(b2f, b2).then_inc(bias_in, 16)
            sp.dma_start(WR[:], wr).then_inc(w_in, 16)
            sp.dma_start(BR[:], br.partition_broadcast(P)).then_inc(w_in, 16)
            sp.dma_start(GM[:], gamma.rearrange("(d o) -> d o", o=1)).then_inc(w_in, 16)
            for i, w in enumerate((wq, wg, wk, wv)):
                sp.dma_start(WA[:, i, :], w).then_inc(w_in, 16)
            sp.dma_start(WA[:, 4:6, :], wa.rearrange("d (a c) -> d a c", a=2)).then_inc(w_in, 16)
            sp.dma_start(WO[:], wo).then_inc(w_in, 16)
            sp.dma_start(X[:, 1, :, :], x_v[1]).then_inc(x_in[1], 16)
            sp.wait_ge(zero_ready, 1)
            for g in range(G):
                half = NT * P * D // (P * T * D)
                for i in range(half):
                    sp.dma_start(rows_in[g][i * P * T:(i + 1) * P * T, :].rearrange("(p t) d -> p (t d)", p=P),
                                 zeros).then_inc(zeroed[g], 16)
                if g == 0:
                    sp.dma_start(W1[:].rearrange("d (e h) -> d e h", e=E), w1.rearrange("e d h -> d e h")).then_inc(ew_in, 16)
                    sp.dma_start(W2[:].rearrange("h (e c o) -> h e c o", e=E, c=2)[:, :, 0, :],
                                 w2.rearrange("e (c h) o -> c h e o", c=2)[0]).then_inc(ew_in, 16)
                    sp.dma_start(W2[:].rearrange("h (e c o) -> h e c o", e=E, c=2)[:, :, 1, :],
                                 w2.rearrange("e (c h) o -> c h e o", c=2)[1]).then_inc(ew_in, 16)
                    sp.wait_ge(parts_ready, 1)
                    sp.dma_start(bias1_parts.rearrange("k e h -> e k h"), b1p).then_inc(parts_out, 16)
                    sp.dma_start(bias2_parts.rearrange("k e h -> e k h"), b2p).then_inc(parts_out, 16)
                    sp.wait_ge(parts_out, 32)
                    sp.dma_start(B1R[:], bias1_parts.rearrange("k e h -> k (e h)")).then_inc(bias_rows, 16)
                    sp.dma_start(B2R[:], bias2_parts.rearrange("k e h -> k (e h)")).then_inc(bias_rows, 16)
                if g + 2 < G:
                    sp.dma_start(X[:, g + 2, :, :], x_v[g + 2]).then_inc(x_in[g + 2], 16)

            def pair_rows(t, i):
                return t[ds(i * 2 * P, 2 * P), :].rearrange("(q p) d -> p q d", p=P)

            def experts(n, f, g):
                def load(i, q, u, waits=True):
                    if waits:
                        sp.wait_ge(xsT_ps, n * NP + i - SLOTS + 1)
                    sp.dma_start(xs[:, u, :, :], pair_rows(rows_in[g], i)).then_inc(xs_in[u], 16)

                def store(i):
                    sp.wait_ge(eo_sb, n * NP + i + 1)

                def put(i, u):
                    store(i)
                    sp.dma_start(pair_rows(rows_out[g], i), eo[:, u, :, :]).then_inc(eo_out[u], 16)

                rn = kind_no[("R", f, g)]
                sp.wait_ge(scattered[rn % 2], 16 * 2 * T * (rn // 2 + 1))
                for i in range(8):
                    load(i, i // SLOTS, i % SLOTS, n > 0 or i >= SLOTS)
                    if i >= 6:
                        put(i - 6, (i - 6) % SLOTS)
                with sp.Fori(2, NP // SLOTS) as q:
                    for u in range(SLOTS):
                        load(q * SLOTS + u, q, u)
                        put(q * SLOTS + (u - 6), (u - 6) % SLOTS)
                for i in range(NP - 6, NP):
                    put(i, i % SLOTS)

            waiting = []
            for st in ORDER:
                if st[0] == "E":
                    experts(kind_no[st], st[1], st[2])
                    for cn, g in waiting:
                        sp.wait_ge(combined, T * (cn + 1))
                        sp.dma_start(out_v[g], X[:, g, :, :]).then_inc(stored, 16)
                    waiting = []
                if st[0] == "C" and st[1] == 1:
                    waiting.append((kind_no[st], st[2]))
            for cn, g in waiting:
                sp.wait_ge(combined, T * (cn + 1))
                sp.dma_start(out_v[g], X[:, g, :, :]).then_inc(stored, 16)
            sp.wait_ge(stored, 16 * G)
            for u in range(SLOTS):
                sp.wait_ge(eo_out[u], 16 * (NP // SLOTS) * 2 * G)

        @block.gpsimd
        def _(pool):
            chain = [0]

            def link(ins):
                chain[0] += 1
                ins.then_inc(pool_chain, 1)
                pool.wait_ge(pool_chain, chain[0])

            link(pool.memset(zeros, 0.0))
            pool.memset(K[:], 0.0).then_inc(zero_ready, 1)
            pool.memset(ones[:], 1.0)
            link(pool.memset(onesf[:], 1.0))
            pool.affine_select(out=ident[:], in_=onesf[:], compare_op=ALU.is_equal, fill=0.0, base=0,
                               pattern=[[-1, P]], channel_multiplier=1)
            pool.affine_select(out=before[:], in_=onesf[:], compare_op=ALU.is_gt, fill=0.0, base=0,
                               pattern=[[1, P]], channel_multiplier=-1)
            link(pool.iota(iota_i[:], [[1, NT]], base=0, channel_multiplier=0))
            link(pool.memset(keep[:], 1.0))
            pool.memset(keep[:, :, 0:1], 0.0)
            pool.tensor_copy(iota_f[:], iota_i[:]).then_inc(consts, 1)

            def scatter(n, f, g):
                pool.wait_ge(rows_ready, n + 1)
                pool.wait_ge(zeroed[g], 16 * (NT // T))
                for j in range(T):
                    for k in range(2):
                        pool.indirect_dma_start(rows_in[g], bass.IndirectOffsetOnAxis(IDX[:, g, j, k:k + 1], 0),
                                                XL[:, n % 2, j, :], None).then_inc(scattered[n % 2], 16)

            def gather(n, en, f, g):
                for u in range(SLOTS):
                    pool.wait_ge(eo_out[u], 16 * (NP // SLOTS) * (en + 1))
                for j in range(T):
                    u = j % SLOTS
                    if n * T + j >= SLOTS:
                        pool.wait_ge(combined, n * T + j - SLOTS + 1)
                    for k in range(2):
                        pool.indirect_dma_start(got[:, u, k, :], None, rows_out[g],
                                                bass.IndirectOffsetOnAxis(IDX[:, g, j, k:k + 1], 0)).then_inc(got_in[u], 16)

            for st in ORDER:
                if st[0] == "R":
                    scatter(kind_no[st], st[1], st[2])
                if st[0] == "C":
                    gather(kind_no[st], kind_no[("E",) + st[1:]], st[1], st[2])

        @block.scalar
        def _(act):
            def route(n, f, g):
                for i in range(4):
                    act.wait_ge(xt_ps, 4 * n + i + 1)
                    act.activation(XT[:, i * 512:(i + 1) * 512], ps[i][:], ACT.Copy).then_inc(xt_sb, 1)
                act.wait_ge(gap_ready, n + 1)
                act.activation(gexp[:], gap[:], ACT.Exp).then_inc(gap_exp, 1)

            def experts(n):
                at = n * NP

                def gelu(m, v):
                    act.wait_ge(hid_ps, at + m + 1)
                    act.activation(hid[:, v, :], ps[2 + v][:], ACT.Gelu).then_inc(hid_sb, 1)

                def move_hidT(m, v):
                    act.wait_ge(hidT_ps, at + m + 1)
                    act.activation(hidT[:, v, :], ps[4 + v][:], ACT.Copy).then_inc(hidT_sb, 1)

                def move_eo(m, u, q=None):
                    act.wait_ge(eo_ps, at + m + 1)
                    if q is not None:
                        act.wait_ge(eo_out[u], 16 * (n * (NP // SLOTS) + q))
                    ins = act.activation(eo[:, u, :, :].rearrange("p a b -> p (a b)"), ps[6 + u % 2][:, 0:256], ACT.Copy)
                    ins.then_inc(eo_sb, 1)
                    return ins

                def move_xsT(m, v):
                    act.wait_ge(xsT_ps, at + m + 1)
                    act.activation(xsT[:, v, :], ps[v][:, 0:256], ACT.Copy).then_inc(xsT_sb, 1)

                def step(m, u, q, static):
                    if not static or m < NP:
                        gelu(m, u % 2)
                    if not static or 1 <= m <= NP:
                        move_hidT(m - 1, (u - 1) % 2)
                    if not static or m >= 2:
                        late = q + (u - 2) // SLOTS
                        move_eo(m - 2, (u - 2) % SLOTS, late if not static or late + n > 0 else None)
                    if not static or m + 2 < NP:
                        move_xsT(m + 2, u % 2)

                move_xsT(0, 0)
                move_xsT(1, 1)
                for m in range(2 * SLOTS):
                    step(m, m % SLOTS, m // SLOTS, True)
                with act.Fori(2, NP // SLOTS - 1) as q:
                    for u in range(SLOTS):
                        step(q * SLOTS + u, u, q, False)
                for m in range(NP - SLOTS, NP + 2):
                    step(m, m % SLOTS, m // SLOTS, True)

            def attention(n, g):
                for i in range(4):
                    act.wait_ge(xnT_ps, 4 * n + i + 1)
                    act.activation(XT[:, i * 512:(i + 1) * 512], ps[i][:], ACT.Copy, scale=GS[:, 0:1]).then_inc(xnT_sb, 1)
                for blk in range(4):
                    cols = slice(blk * 512, (blk + 1) * 512)
                    steps = slice(blk * 4, blk * 4 + 4)

                    def bank(w):
                        return ps[(4 + blk * 6 + w) % 8]

                    def there(w):
                        act.wait_ge(proj_ps, 24 * n + 6 * blk + w + 1)

                    there(0)
                    act.activation(qg[:, cols], bank(0)[:], ACT.Copy).then_inc(proj_act, 1)
                    there(1)
                    act.activation(tmp[3][:, cols], bank(1)[:], ACT.Copy).then_inc(proj_act, 1)
                    there(2)
                    act.activation(kv[:, cols], bank(2)[:], ACT.Copy).then_inc(proj_act, 1)
                    there(4)
                    act.activation(cr[:, steps, :].rearrange("p a b -> p (a b)"), bank(4)[:], ACT.Copy)
                    act.activation(tmp[0][:, cols], bank(4)[:], ACT.Square).then_inc(proj_act, 1)
                    there(5)
                    act.activation(ci[:, steps, :].rearrange("p a b -> p (a b)"), bank(5)[:], ACT.Copy)
                    act.activation(tmp[1][:, cols], bank(5)[:], ACT.Square).then_inc(proj_act, 1)
                act.wait_ge(r2_ready, n + 1)
                act.activation(tmp[2], tmp[0], ACT.Sqrt).then_inc(r_ready, 1)
                act.wait_ge(r_ready, n + 1)
                act.activation(tmp[1], tmp[2], ACT.Sigmoid).then_inc(m_ready, 1)
                act.activation(XT[:], tmp[3], ACT.Silu).then_inc(sg_ready, 1)

            act.wait_ge(w_in, small_weights)
            act.activation(GS[:], GM[:], ACT.Copy, scale=float(D) ** 0.5).then_inc(gs_ready, 1)
            act.wait_ge(gs_ready, 1)
            for st in ORDER:
                if st[0] == "R":
                    route(kind_no[st], st[1], st[2])
                if st[0] == "E":
                    experts(kind_no[st])
                if st[0] == "A":
                    attention(kind_no[st], st[1])

        @block.tensor
        def _(pe):
            def free_banks(st):
                old = psum_before[st]
                if old is None:
                    return
                done = kind_no[old] + 1
                if old[0] == "R":
                    pe.wait_ge(rank_read, done)
                if old[0] == "E":
                    pe.wait_ge(eo_sb, NP * done)
                if old[0] == "A":
                    pe.wait_ge(proj_act, 20 * done)
                    pe.wait_ge(proj_dve, 4 * done)
                if old[0] == "A3":
                    pe.wait_ge(x_added, 4 * done)

            def route(st, n):
                free_banks(st)
                if n == 0:
                    pe.wait_ge(consts, 1)
                for i in range(4):
                    pe.wait_ge(xl_ready, 4 * n + i + 1)
                    for j in range(4):
                        ins = pe.transpose(ps[i][:, j * P:(j + 1) * P], XL[:, n % 2, 4 * i + j, :], ident[:])
                    ins.then_inc(xt_ps, 1)
                if n == 0:
                    pe.wait_ge(w_in, small_weights)
                for j in range(T):
                    if j % 4 == 0:
                        pe.wait_ge(xt_sb, 4 * n + j // 4 + 1)
                    ins = pe.matmul(ps[4][:, j * E:(j + 1) * E], XT[:, j * P:(j + 1) * P], WR[:], start=True, stop=True)
                ins.then_inc(logits_ps, 1)
                pe.wait_ge(mask_ready, n + 1)
                flat = mask[:].rearrange("p t e -> p (t e)")
                pe.matmul(ps[5][:, 0:T * E], before[:], flat, start=True, stop=True)
                pe.matmul(ps[5][:, T * E:2 * T * E], ones[:], flat, start=True, stop=True).then_inc(rank_ps, 1)

            def experts(st, n, f, g):
                at = n * NP
                free_banks(st)
                pe.wait_ge(rows_ready, kind_no[("R", f, g)] + 1)
                if n == 0:
                    pe.wait_ge(bias_rows, 32)
                    pe.wait_ge(ew_in, expert_weights)

                def expert(m, q):
                    return pe.value_load(TE[0:1, g, ds(2 * m + q, 1)], min_val=0, max_val=E - 1)

                def turn_x(m, u, q):
                    pe.wait_ge(xs_in[u], 16 * (n * (NP // SLOTS) + q + 1))
                    for a in range(2):
                        ins = pe.transpose(ps[u % 2][:, a * P:(a + 1) * P], xs[:, u, a, :], ident[:])
                    ins.then_inc(xsT_ps, 1)

                def up(m, v):
                    pair = [expert(m, a) for a in range(2)]
                    pe.wait_ge(xsT_sb, at + m + 1)
                    for a, e in enumerate(pair):
                        o = ps[2 + v][:, a * H:(a + 1) * H]
                        pe.matmul(o, xsT[:, v, a * P:(a + 1) * P], W1[:, ds(e * H, H)], start=True, stop=False)
                        ins = pe.matmul(o, ones[0:3, :], B1R[:, ds(e * H, H)], start=False, stop=True)
                    ins.then_inc(hid_ps, 1)

                def turn_h(m, v):
                    pe.wait_ge(hid_sb, at + m + 1)
                    for a in range(4):
                        ins = pe.transpose(ps[4 + v][:, a * P:(a + 1) * P], hid[:, v, a * P:(a + 1) * P], ident[:])
                    ins.then_inc(hidT_ps, 1)

                def down(m, v, old):
                    pair = [expert(m, a) for a in range(2)]
                    pe.wait_ge(hidT_sb, at + m + 1)
                    if old:
                        pe.wait_ge(eo_sb, at + m - 1)
                    for a, e in enumerate(pair):
                        o = ps[6 + v][:, a * D:(a + 1) * D]
                        for c in range(2):
                            pe.matmul(o, hidT[:, v, (2 * a + c) * P:(2 * a + c + 1) * P],
                                      W2[:, ds(e * H + c * D, D)], start=(c == 0), stop=False)
                        ins = pe.matmul(o, ones[0:3, :], B2R[:, ds(e * D, D)], start=False, stop=True)
                    ins.then_inc(eo_ps, 1)

                def step(m, u, q, static):
                    if not static or m < NP:
                        up(m, u % 2)
                    if not static or 1 <= m <= NP:
                        turn_h(m - 1, (u - 1) % 2)
                    if not static or m >= 2:
                        down(m - 2, u % 2, not static or m >= 4)
                    if not static or m + 2 < NP:
                        turn_x(m + 2, (u + 2) % SLOTS, q + (u + 2) // SLOTS)

                turn_x(0, 0, 0)
                turn_x(1, 1, 0)
                for m in range(SLOTS):
                    step(m, m, 0, True)
                with pe.Fori(1, NP // SLOTS - 1) as q:
                    for u in range(SLOTS):
                        step(q * SLOTS + u, u, q, False)
                for m in range(NP - SLOTS, NP + 2):
                    step(m, m % SLOTS, m // SLOTS, True)

            def attention(st, n, g):
                free_banks(st)
                for i in range(4):
                    pe.wait_ge(xn_ready, 4 * n + i + 1)
                    for j in range(4):
                        ins = pe.transpose(ps[i][:, j * P:(j + 1) * P], XN[:, 4 * i + j, :], ident[:])
                    ins.then_inc(xnT_ps, 1)
                for blk in range(4):
                    pe.wait_ge(xnT_sb, 4 * n + blk + 1)
                    for w in range(6):
                        k = blk * 6 + w
                        if 4 + k - 8 >= 0 and k < 8:
                            pe.wait_ge(xnT_sb, 4 * n + min(k - 3, 4))
                        if k >= 8:
                            old = k - 8
                            if old % 6 == 3:
                                pe.wait_ge(proj_dve, 4 * n + old // 6 + 1)
                            else:
                                pe.wait_ge(proj_act, 20 * n + 5 * (old // 6) + [1, 2, 3, 0, 4, 5][old % 6])
                        pe.matmul(ps[(4 + k) % 8][:], WA[:, w, :], XT[:, blk * 512:(blk + 1) * 512],
                                  start=True, stop=True).then_inc(proj_ps, 1)

            def project(st, n, g):
                free_banks(st)
                pe.wait_ge(y_ready, n + 1)
                for i in range(4):
                    for j in range(4):
                        ins = pe.matmul(ps[i][:, j * D:(j + 1) * D], kv[:, (4 * i + j) * P:(4 * i + j + 1) * P], WO[:],
                                        start=True, stop=True)
                    ins.then_inc(wo_ps, 1)

            for st in ORDER:
                if st[0] == "R":
                    route(st, kind_no[st])
                if st[0] == "E":
                    experts(st, kind_no[st], st[1], st[2])
                if st[0] == "A":
                    attention(st, kind_no[st], st[1])
                if st[0] == "A3":
                    project(st, kind_no[st], st[1])

        @block.vector
        def _(dve):
            chain = [0]

            def link(ins, times=1):
                chain[0] += times
                ins.then_inc(dve_chain, 1)
                dve.wait_ge(dve_chain, chain[0])

            def norm(g, out, for_attention, ready):
                with dve.Fori(0, T // 4) as i:
                    for u in range(4):
                        ins = dve.bn_stats(stats[:, ds(i * 4 + u, 1), :].rearrange("p a b -> p (a b)"),
                                           X[:, g, ds(i * 4 + u, 1), :].rearrange("p a b -> p (a b)"))
                    ins.then_inc(dve_chain, 1)
                chain[0] += T // 4
                dve.wait_ge(dve_chain, chain[0])
                dve.tensor_tensor(m2[:], stats[:, :, 1], stats[:, :, 4], add)
                dve.tensor_tensor(df[:], stats[:, :, 1], stats[:, :, 4], sub)
                link(dve.tensor_tensor(var[:], stats[:, :, 2], stats[:, :, 5], add))
                link(dve.scalar_tensor_tensor(out=df[:], in0=df[:], scalar=0.25, in1=df[:], op0=mult, op1=mult))
                link(dve.scalar_tensor_tensor(out=var[:], in0=var[:], scalar=1.0 / D, in1=df[:], op0=mult, op1=add))
                if for_attention:
                    link(dve.tensor_scalar(var[:], var[:], float(D) + EPS, EPS * EPS, mult, add))
                else:
                    link(dve.tensor_scalar(var[:], var[:], EPS, None, add))
                dve.tensor_scalar(vh[:], var[:], -0.5, None, mult)
                link(dve.tensor_scalar(seed[:], var[:].bitcast(u32), 1, None, ALU.logical_shift_right))
                link(dve.tensor_scalar(rs[:].bitcast(i32), seed[:], -1.0, float(0x5f3759df), mult, add))
                for _ in range(3):
                    link(dve.tensor_tensor(na[:], rs[:], rs[:], mult))
                    link(dve.tensor_tensor(na[:], na[:], vh[:], mult))
                    link(dve.scalar_tensor_tensor(out=rs[:], in0=na[:], scalar=1.5, in1=rs[:], op0=add, op1=mult))
                link(dve.scalar_tensor_tensor(out=nb[:], in0=m2[:], scalar=-0.5, in1=rs[:], op0=mult, op1=mult))
                with dve.Fori(0, T // 4) as i:
                    for u in range(4):
                        j = ds(i * 4 + u, 1)
                        ins = dve.tensor_scalar(out[:, j, :].rearrange("p a b -> p (a b)"),
                                                X[:, g, j, :].rearrange("p a b -> p (a b)"),
                                                rs[:, j], nb[:, j], mult, add)
                    ins.then_inc(ready, 1)

            def route(n, f, g):
                if f == 0:
                    dve.wait_ge(x_in[g], 16)
                if n >= 2:
                    dve.wait_ge(scattered[n % 2], 16 * 2 * T * (n // 2))
                xl = XL[:, n % 2, :, :]
                norm(g, xl, False, xl_ready)
                dve.wait_ge(xl_ready, (T // 4) * (n + 1))
                xg = X[:, g, :, :].rearrange("p t d -> p (t d)")
                link(dve.scalar_tensor_tensor(out=xg, in0=xl.rearrange("p t d -> p (t d)"), scalar=0.5, in1=xg,
                                              op0=mult, op1=add))
                dve.wait_ge(logits_ps, n + 1)
                link(dve.tensor_tensor(LG[:], ps[4][:, 0:T * E].rearrange("p (t e) -> p t e", t=T),
                                       BR[:].unsqueeze(1).broadcast_to([P, T, E]), add))
                for j in range(T):
                    ins = dve.max(MX[:, j, :], LG[:, j, :])
                link(ins)
                dve.tensor_tensor(gap[:], MX[:, :, 1], MX[:, :, 0], sub).then_inc(gap_ready, 1)
                for j in range(T):
                    ins = dve.max_index(IX[:, j, :], MX[:, j, :], LG[:, j, :])
                link(ins)
                link(dve.tensor_copy(IXF[:], IX[:, :, 0:2]))
                for k in range(2):
                    ins = dve.tensor_tensor(hot[:, k, :, :], iota_f[:, 0:E].unsqueeze(1).broadcast_to([P, T, E]),
                                            IXF[:, :, k:k + 1].broadcast_to([P, T, E]), ALU.is_equal)
                link(ins)
                dve.tensor_tensor(mask[:], hot[:, 0, :, :], hot[:, 1, :, :], add).then_inc(mask_ready, 1)
                dve.wait_ge(gap_exp, n + 1)
                link(dve.tensor_scalar(den[:], gexp[:], 1.0, None, add))
                link(dve.reciprocal(den[:], den[:]))
                link(dve.tensor_scalar(WGT[:, g, 0, :], den[:], 0.5, None, mult))
                dve.tensor_tensor(WGT[:, g, 1, :], WGT[:, g, 0, :], gexp[:], mult)
                link(dve.memset(cnt[:, :, 0:1], 0.0))
                dve.wait_ge(rank_ps, n + 1)
                link(dve.tensor_copy(cnt[:, :, 1:T + 1], ps[5][:, T * E:2 * T * E].rearrange("p (t e) -> p e t", t=T)))
                link(dve.tensor_tensor_scan(off[:].rearrange("p e t -> p (e t)"), keep[:].rearrange("p e t -> p (e t)"),
                                            cnt[:].rearrange("p e t -> p (e t)"), 0.0, mult, add))
                link(dve.tensor_scalar(nte[:], off[:, :, T:T + 1].rearrange("p e o -> p (e o)"), 1.0 / P, 127.0 / 256.0, mult, add))
                link(dve.tensor_scalar(nte[:], nte[:], 12582912.0, -12582912.0, add, add))
                link(dve.tensor_tensor_scan(cum[:], onesf[:, 0:E], nte[:], 0.0, mult, add))
                link(dve.tensor_tensor(basee[:], cum[:], nte[:], sub))
                link(dve.scalar_tensor_tensor(out=off[:, :, 0:T], in0=basee[:].unsqueeze(2).broadcast_to([P, E, T]),
                                              scalar=float(P), in1=off[:, :, 0:T], op0=mult, op1=add))
                ins = dve.tensor_tensor(pos[:], ps[5][:, 0:T * E].rearrange("p (t e) -> p t e", t=T),
                                        off[:, :, 0:T].rearrange("p e t -> p t e"), add)
                ins.then_inc(rank_read, 1)
                dve.wait_ge(rank_read, n + 1)
                for k in range(2):
                    ins = dve.tensor_tensor(sel[:, k, :, :], hot[:, k, :, :], pos[:], mult)
                link(ins)
                for k in range(2):
                    ins = dve.tensor_reduce(rowf[:, :, k:k + 1], sel[:, k, :, :], AX.X, add)
                link(ins)
                dve.tensor_copy(IDX[:, g, :, :], rowf[:])
                link(dve.tensor_tensor(tcmp, iota_f[0:1, :].unsqueeze(2).broadcast_to([1, NT, E]),
                                       cum[0:1, :].unsqueeze(1).broadcast_to([1, NT, E]), ALU.is_ge))
                link(dve.tensor_reduce(tef[:].unsqueeze(2), tcmp, AX.X, add))
                dve.tensor_scalar(TE[0:1, g, :], tef[:], float(E - 1), None, ALU.min).then_inc(rows_ready, 1)

            def combine(n, g):
                with dve.Fori(0, T // SLOTS) as q:
                    for u in range(SLOTS):
                        dve.wait_ge(got_in[u], q * 32 + 32 * (n * (T // SLOTS) + 1))
                    for k in range(2):
                        for u in range(SLOTS):
                            j = ds(q * SLOTS + u, 1)
                            xt = X[:, g, j, :].rearrange("p a b -> p (a b)")
                            ins = dve.scalar_tensor_tensor(out=xt, in0=got[:, u, k, :], scalar=WGT[:, g, k, j], in1=xt,
                                                           op0=mult, op1=add)
                            if k == 1:
                                ins.then_inc(combined, 1)
                        if k == 0:
                            ins.then_inc(dve_chain, 1)
                            dve.wait_ge(dve_chain, q + (chain[0] + 1))
                chain[0] += T // SLOTS
                dve.wait_ge(combined, T * (n + 1))

            def attention(n, g):
                if n == 0:
                    for i in range(G):
                        dve.wait_ge(zeroed[i], 16 * (NT // T))
                norm(g, XN, True, xn_ready)
                for blk in range(4):
                    cols = slice(blk * 512, (blk + 1) * 512)
                    dve.wait_ge(proj_act, 20 * n + 5 * blk + 3)
                    dve.wait_ge(proj_ps, 24 * n + 6 * blk + 4)
                    dve.tensor_tensor(kv[:, cols], ps[(4 + blk * 6 + 3) % 8][:], kv[:, cols], mult).then_inc(proj_dve, 1)
                dve.wait_ge(proj_act, 20 * (n + 1))
                crf, cif = cr[:].rearrange("p l c -> p (l c)"), ci[:].rearrange("p l c -> p (l c)")
                dve.scalar_tensor_tensor(out=tmp[0], in0=tmp[0], scalar=TINY * TINY, in1=tmp[1],
                                         op0=add, op1=add).then_inc(r2_ready, 1)
                dve.wait_ge(r_ready, n + 1)
                link(dve.reciprocal(tmp[0], tmp[2]))
                dve.wait_ge(m_ready, n + 1)
                link(dve.tensor_tensor(tmp[0], tmp[0], tmp[1], mult))
                dve.scalar_tensor_tensor(out=crf, in0=crf, scalar=TINY, in1=tmp[0], op0=add, op1=mult)
                dve.tensor_tensor(cif, cif, tmp[0], mult)
                dve.wait_ge(sg_ready, n + 1)
                link(dve.tensor_tensor(qg[:], qg[:], XT[:], mult))

            def scan(n):
                dve.tensor_copy(S[:, 0, 0, :], kv[:, 0:P])
                dve.memset(S[:, 0, 1, :], 0.0)
                dve.tensor_copy(S[:, 0, 2, :], cr[:, 0, :])
                link(dve.tensor_copy(S[:, 0, 3, :], ci[:, 0, :]))
                start = chain[0]
                with dve.Fori(1, T) as l:
                    old = S[:, ds(l - 1, 1), :, :].rearrange("p o f c -> p (o f) c")
                    new = S[:, ds(l, 1), :, :].rearrange("p o (a r) c -> p (o a) r c", a=2)
                    dve.tensor_tensor(t1.rearrange("p a r c -> p (a r) c"),
                                      cr[:, ds(l, 1), :].broadcast_to([P, 4, P]), old, mult)
                    dve.tensor_tensor(t2.rearrange("p a r c -> p (a r) c"),
                                      ci[:, ds(l, 1), :].broadcast_to([P, 4, P]), old, mult).then_inc(dve_chain, 1)
                    dve.wait_ge(dve_chain, l * 3 + (start - 2))
                    dve.tensor_tensor(new[:, :, 0, :], t1[:, :, 0, :], t2[:, :, 1, :], sub).then_inc(dve_chain, 1)
                    dve.tensor_tensor(new[:, :, 1, :], t1[:, :, 1, :], t2[:, :, 0, :], add)
                    dve.wait_ge(dve_chain, l * 3 + (start - 1))
                    hr = S[:, ds(l, 1), 0, :].rearrange("p o c -> p (o c)")
                    dve.tensor_tensor(hr, hr, kv[:, ds(l * P, P)], add).then_inc(dve_chain, 1)
                    dve.wait_ge(dve_chain, l * 3 + start)
                chain[0] += 3 * (T - 1)
                end = S[:, T - 1, :, :].rearrange("p f (b c) -> p f b c", b=BG)
                link(dve.tensor_copy(K[:, :, :, 1], end[:, 0:2, :, 0]))
                for c in range(1, C - 1):
                    dve.tensor_tensor(k1[:], end[:, 2:3, :, c].broadcast_to([P, 2, BG]), K[:, :, :, c], mult)
                    link(dve.tensor_tensor(k2[:], end[:, 3:4, :, c].broadcast_to([P, 2, BG]), K[:, :, :, c], mult))
                    link(dve.tensor_tensor(k1[:], k1[:], end[:, 0:2, :, c], add))
                    dve.tensor_tensor(K[:, 0, :, c + 1], k1[:, 0, :], k2[:, 1, :], sub)
                    link(dve.tensor_tensor(K[:, 1, :, c + 1], k1[:, 1, :], k2[:, 0, :], add))
                kr = K[:, 0, :, :].rearrange("p b c -> p (b c)").unsqueeze(1).broadcast_to([P, T, P])
                ki = K[:, 1, :, :].rearrange("p b c -> p (b c)").unsqueeze(1).broadcast_to([P, T, P])
                dve.tensor_tensor(S[:, :, 2, :], S[:, :, 2, :], kr, mult)
                link(dve.tensor_tensor(S[:, :, 3, :], S[:, :, 3, :], ki, mult))
                link(dve.tensor_tensor(S[:, :, 0, :], S[:, :, 0, :], S[:, :, 2, :], add))
                link(dve.tensor_tensor(S[:, :, 0, :], S[:, :, 0, :], S[:, :, 3, :], sub))
                dve.tensor_tensor(kv[:].rearrange("p (l c) -> p l c", l=T), S[:, :, 0, :],
                                  qg[:].rearrange("p (l c) -> p l c", l=T), mult).then_inc(y_ready, 1)

            def add_attention(n, g):
                for i in range(4):
                    dve.wait_ge(wo_ps, 4 * n + i + 1)
                    xq = X[:, g, 4 * i:4 * i + 4, :].rearrange("p t d -> p (t d)")
                    dve.tensor_tensor(xq, ps[i][:], xq, add).then_inc(x_added, 1)
                dve.wait_ge(x_added, 4 * (n + 1))

            dve.wait_ge(bias_in, 32)
            for k in range(3):
                if k < 2:
                    dve.tensor_copy(b1p[:, k, :], b1f)
                link(dve.tensor_copy(b2p[:, k, :], b2f))
                if k < 2:
                    dve.tensor_tensor(b1f, b1f, b1p[:, k, :], sub)
                    link(dve.tensor_tensor(b2f, b2f, b2p[:, k, :], sub))
            dve.tensor_copy(b1p[:, 2, :], b1f).then_inc(parts_ready, 1)
            dve.wait_ge(consts, 1)
            dve.wait_ge(w_in, small_weights)
            for st in ORDER:
                if st[0] == "R":
                    route(kind_no[st], st[1], st[2])
                if st[0] == "C":
                    combine(kind_no[st], st[2])
                if st[0] == "A":
                    attention(kind_no[st], st[1])
                if st[0] == "A2":
                    scan(kind_no[st])
                if st[0] == "A3":
                    add_attention(kind_no[st], st[1])


_INS = ["L0_attn_x", "L0_attn_gamma", "L0_attn_wq", "L0_attn_wk", "L0_attn_wv", "L0_attn_wa", "L0_attn_wg", "L0_attn_wo",
        "L0_ffn_Wr", "L0_ffn_br", "L0_ffn_W1", "L0_ffn_b1", "L0_ffn_W2", "L0_ffn_b2"]


def kernel(**inputs):
    import numpy as np
    import concourse.bacc as bacc
    from concourse.bass_utils import run_bass_kernel_spmd as run

    nc = bacc.Bacc("TRN2", target_bir_lowering=False, num_devices=1)
    arrays, args = {}, []
    for name in _INS:
        a = np.ascontiguousarray(inputs[name])
        arrays["in_" + name] = a
        args.append(nc.dram_tensor("in_" + name, a.shape, mybir.dt.from_np(a.dtype), kind="ExternalInput").ap())
    args.append(nc.dram_tensor("out_0", (B, N, D), mybir.dt.float32, kind="ExternalOutput").ap())
    build(nc, *args)
    return run(nc, [arrays], core_ids=[0]).results[0]["out_0"]
```

```python
import concourse.bass as bass
from concourse import mybir
from contextlib import ExitStack

P = 128
D = 128
B, N = 32, 256
E, H = 16, 256
G = 4
T = B * N // G // P
C = N // T
BG = B // G
NT = 2 * T + E
NP = NT // 2
SLOTS = 4
XBUF = 3
RING = 8
EPS = 1e-5
TINY = 1e-18

ORDER = [("N", (0, 0), None), ("R", 0, 0), ("K", 0, 0), ("N", (0, 1), None), ("R", 0, 1), ("K", 0, 1), ("E", 0, 0),
         ("N", (0, 2), None), ("R", 0, 2), ("G", 0, 0), ("K", 0, 2), ("C", 0, 0),
         ("N", (0, 3), 0), ("R", 0, 3), ("A", 0), ("K", 0, 3), ("A1", 0), ("E", 0, 1), ("E", 0, 2), ("A2", 0),
         ("G", 0, 1), ("C", 0, 1), ("A3", 0),
         ("N", (1, 0), 1), ("R", 1, 0), ("A", 1), ("K", 1, 0), ("A1", 1), ("E", 0, 3), ("A2", 1), ("G", 0, 2), ("C", 0, 2),
         ("A3", 1),
         ("N", (1, 1), 2), ("R", 1, 1), ("A", 2), ("K", 1, 1), ("A1", 2), ("E", 1, 0), ("A2", 2), ("G", 0, 3), ("C", 0, 3),
         ("A3", 2),
         ("N", (1, 2), 3), ("R", 1, 2), ("A", 3), ("K", 1, 2), ("A1", 3), ("E", 1, 1), ("A2", 3), ("G", 1, 0), ("C", 1, 0),
         ("A3", 3),
         ("N", (1, 3), None), ("R", 1, 3), ("K", 1, 3), ("E", 1, 2), ("G", 1, 1), ("C", 1, 1), ("E", 1, 3),
         ("G", 1, 2), ("C", 1, 2), ("G", 1, 3), ("C", 1, 3)]


def build(nc, x, gamma, wq, wk, wv, wa, wg, wo, wr, br, w1, b1, w2, b2, out):
    f32, bf16, i32, u32 = mybir.dt.float32, mybir.dt.bfloat16, mybir.dt.int32, mybir.dt.uint32
    ALU = mybir.AluOpType
    ACT = mybir.ActivationFunctionType
    AX = mybir.AxisListType
    ds = bass.ds
    add, sub, mult = ALU.add, ALU.subtract, ALU.mult

    x_v = x.rearrange("(g b) (c l) d -> g (b c) l d", g=G, l=T)
    out_v = out.rearrange("(g b) (c l) d -> g (b c) l d", g=G, l=T)
    rows_in = [nc.dram_tensor(f"rows_in{g}", (NT * P, D), f32, kind="Internal").ap() for g in range(G)]
    rows_out = [nc.dram_tensor(f"rows_out{g}", (NT * P, D), f32, kind="Internal").ap() for g in range(G)]
    up_weights = nc.dram_tensor("up_weights", (E, D, H + 2), f32, kind="Internal").ap()
    bias2_parts = nc.dram_tensor("bias2_parts", (3, E, D), bf16, kind="Internal").ap()

    kind_no = {}
    psum_before = {}
    seen, last = {}, None
    for st in ORDER:
        kind_no[st] = seen.get(st[0], 0)
        seen[st[0]] = kind_no[st] + 1
        psum_before[st] = last
        if st[0] in ("R", "K", "E", "A", "A3"):
            last = st

    with ExitStack() as ctx:
        def sb(name, shape, dt):
            return ctx.enter_context(nc.sbuf_tensor(name, shape, dt))

        def sem(name):
            return ctx.enter_context(nc.semaphore(name))

        X = sb("X", [P, G, T, D], f32)
        XL = sb("XL", [P, XBUF, T, D], f32)
        WUP = sb("WUP", [P, SLOTS, 2, H + 2], f32)
        W2 = sb("W2", [P, E * H], f32)
        B2R = sb("B2R", [3, E * D], bf16)
        WA = sb("WA", [P, 6, D], f32)
        WO = sb("WO", [P, D], f32)
        WR = sb("WR", [P, E], f32)
        BR = sb("BR", [P, E], f32)
        GM = sb("GM", [P, 1], f32)
        GS = sb("GS", [P, 1], f32)
        ident = sb("ident", [P, P], f32)
        onesf = sb("onesf", [P, P], f32)
        before = sb("before", [P, P], bf16)
        ones = sb("ones", [P, P], bf16)
        iota_i = sb("iota_i", [P, NT], i32)
        iota_f = sb("iota_f", [P, NT], f32)
        keep = sb("keep", [P, E, T + 1], f32)
        IDX = sb("IDX", [P, G, T, 2], u32)
        WGT = sb("WGT", [P, G, 2, T], f32)
        TE2 = sb("TE2", [1, G, NP], i32)
        TE4 = sb("TE4", [1, G, NP // 2], i32)
        stats = sb("stats", [P, 2 * T, 6], f32)
        m2 = sb("m2", [P, 2 * T], f32)
        df = sb("df", [P, 2 * T], f32)
        var = sb("var", [P, 2 * T], f32)
        vh = sb("vh", [P, 2 * T], f32)
        seed = sb("seed", [P, 2 * T], u32)
        rs = sb("rs", [P, 2 * T], f32)
        na = sb("na", [P, 2 * T], f32)
        nb = sb("nb", [P, 2 * T], f32)
        XT = sb("XT", [P, T * D], f32)
        LG = sb("LG", [P, T, E], f32)
        MX = sb("MX", [P, T, 8], f32)
        IX = sb("IX", [P, T, 8], u32)
        IXF = sb("IXF", [P, T, 2], f32)
        gap = sb("gap", [P, T], f32)
        gexp = sb("gexp", [P, T], f32)
        den = sb("den", [P, T], f32)
        mask = sb("mask", [P, T, E], bf16)
        cnt = sb("cnt", [P, E, T + 1], f32)
        off = sb("off", [P, E, T + 1], f32)
        nte = sb("nte", [P, E], f32)
        cum = sb("cum", [P, E], f32)
        basee = sb("basee", [P, E], f32)
        pos = sb("pos", [P, T, E], f32)
        rowf = sb("rowf", [P, T, 2], f32)
        tef = sb("tef", [1, NT], f32)
        tep = sb("tep", [1, NP], f32)
        xs = sb("xs", [P, 2, 4, D], f32)
        xsT = sb("xsT", [P, 2, 2 * P], f32)
        hidT = sb("hidT", [P, 2, 4 * P], f32)
        eo = sb("eo", [P, 2, 4, D], f32)
        got = sb("got", [P, RING, 2, D], f32)
        kv = sb("kv", [P, T * P], f32)
        cr = sb("cr", [P, T, P], f32)
        ci = sb("ci", [P, T, P], f32)
        qg = sb("qg", [P, T * P], f32)
        S = sb("S", [P, T, 4, P], f32)
        scratch = sb("scratch", [P, 1024], f32)
        Y = sb("Y", [P, 4, BG, C], f32)
        S_flat = S[:].rearrange("p l f c -> p (l f c)")
        W = T * P
        tmp = [S_flat[:, i * W:(i + 1) * W] for i in range(4)]
        XN = kv[:].rearrange("p (l d) -> p l d", l=T)
        zeros = kv[:]
        b2f = S_flat[0:E, 0:D]
        b2p = S_flat[0:E, 1024:2048].bitcast(bf16)[:, 0:3 * D].rearrange("e (k h) -> e k h", k=3)
        hot = scratch[:, 0:512].rearrange("p (k t e) -> p k t e", k=2, t=T)
        sel = scratch[:, 512:1024].rearrange("p (k t e) -> p k t e", k=2, t=T)
        tcmp = scratch[0:1, 0:NT * E].rearrange("p (t e) -> p t e", t=NT)
        t1 = scratch[:, 0:512].rearrange("p (f c) -> p f c", f=4)
        t2 = scratch[:, 512:1024].rearrange("p (f c) -> p f c", f=4)
        ps = [ctx.enter_context(nc.psum_tensor(f"bank{i}", [P, 512], f32)) for i in range(8)]

        x_in = [sem(f"x_in{g}") for g in range(G)]
        zeroed = [sem(f"zeroed{g}") for g in range(G)]
        w_in, down_in, up_put = sem("w_in"), sem("down_in"), sem("up_put")
        bias_in, parts_out, bias_rows = sem("bias_in"), sem("parts_out"), sem("bias_rows")
        consts, zero_ready, parts_ready = sem("consts"), sem("zero_ready"), sem("parts_ready")
        dve_chain, pool_chain = sem("dve_chain"), sem("pool_chain")
        rank_read, x_added, gs_ready = sem("rank_read"), sem("x_added"), sem("gs_ready")
        xl_ready, xt_ps, xt_sb, logits_ps = sem("xl_ready"), sem("xt_ps"), sem("xt_sb"), sem("logits_ps")
        gap_ready, gap_exp, mask_ready, rank_ps, rows_ready = (sem("gap_ready"), sem("gap_exp"), sem("mask_ready"),
                                                             sem("rank_ps"), sem("rows_ready"))
        scattered = [sem(f"scattered{i}") for i in range(XBUF)]
        norm_ready, logits_read = sem("norm_ready"), sem("logits_read")
        xs_in = [sem(f"xs_in{i}") for i in range(2)]
        eo_out = [sem(f"eo_out{i}") for i in range(2)]
        up_in = [sem(f"up_in{i}") for i in range(SLOTS)]
        xsT_ps, xsT_sb, hid_ps, hid_sb = sem("xsT_ps"), sem("xsT_sb"), sem("hid_ps"), sem("hid_sb")
        eo_ps, eo_sb = sem("eo_ps"), sem("eo_sb")
        got_in = [sem(f"got_in{i}") for i in range(RING)]
        combined = sem("combined")
        xn_ready, xnT_ps, xnT_sb = sem("xn_ready"), sem("xnT_ps"), sem("xnT_sb")
        proj_ps, proj_act, proj_dve = sem("proj_ps"), sem("proj_act"), sem("proj_dve")
        r2_ready, r_ready, log_ready, inv_ready = sem("r2_ready"), sem("r_ready"), sem("log_ready"), sem("inv_ready")
        m_ready, sg_ready = sem("m_ready"), sem("sg_ready")
        y_ready, wo_ps, stored = sem("y_ready"), sem("wo_ps"), sem("stored")

        block = ctx.enter_context(nc.Block())
        small_weights, down_weights, up_parts = 9 * 16, 2 * 16, 3 * 16

        @block.sync
        def _(sp):
            sp.dma_start(X[:, 0, :, :], x_v[0]).then_inc(x_in[0], 16)
            sp.dma_start(b2f, b2).then_inc(bias_in, 16)
            sp.dma_start(WR[:], wr).then_inc(w_in, 16)
            sp.dma_start(BR[:], br.partition_broadcast(P)).then_inc(w_in, 16)
            sp.dma_start(GM[:], gamma.rearrange("(d o) -> d o", o=1)).then_inc(w_in, 16)
            for i, w in enumerate((wq, wg, wk, wv)):
                sp.dma_start(WA[:, i, :], w).then_inc(w_in, 16)
            sp.dma_start(WA[:, 4:6, :], wa.rearrange("d (a c) -> d a c", a=2)).then_inc(w_in, 16)
            sp.dma_start(WO[:], wo).then_inc(w_in, 16)
            sp.dma_start(up_weights[:, :, 0:H], w1).then_inc(up_put, 16)
            for c in range(2):
                sp.dma_start(up_weights[:, :, H + c:H + c + 1],
                             b1[:, c * P:(c + 1) * P].rearrange("e (p o) -> e p o", o=1),
                             allow_slow_non_contiguous=True).then_inc(up_put, 16)
            sp.dma_start(X[:, 1, :, :], x_v[1]).then_inc(x_in[1], 16)
            sp.wait_ge(zero_ready, 1)
            for g in range(G):
                for i in range(NT // T):
                    sp.dma_start(rows_in[g][i * P * T:(i + 1) * P * T, :].rearrange("(p t) d -> p (t d)", p=P),
                                 zeros).then_inc(zeroed[g], 16)
                if g == 0:
                    for c in range(2):
                        sp.dma_start(W2[:].rearrange("h (e c o) -> h e c o", e=E, c=2)[:, :, c, :],
                                     w2.rearrange("e (c h) o -> c h e o", c=2)[c]).then_inc(down_in, 16)
                    sp.wait_ge(parts_ready, 1)
                    sp.dma_start(bias2_parts.rearrange("k e h -> e k h"), b2p).then_inc(parts_out, 16)
                    sp.wait_ge(parts_out, 16)
                    sp.dma_start(B2R[:], bias2_parts.rearrange("k e h -> k (e h)")).then_inc(bias_rows, 16)
                if g + 2 < G:
                    sp.dma_start(X[:, g + 2, :, :], x_v[g + 2]).then_inc(x_in[g + 2], 16)
            sp.wait_ge(up_put, up_parts)

            def experts(n, f, g):
                rn = kind_no[("R", f, g)]

                def load_rows(d, old=True):
                    if old:
                        sp.wait_ge(xsT_ps, n * NP - 2 + d * 2)

                def load_weights(d, v, old=True):
                    words = sp.value_load(TE4[0:1, g, ds(d, 1)], min_val=0, max_val=E ** 4 - 1)
                    for h in range(2):
                        u = 2 * v + h
                        if old:
                            sp.wait_ge(hid_sb, n * NP + (h - 3) + d * 2)
                        for a in range(2):
                            e = (words // E ** (2 * h + a)) % E if 2 * h + a < 3 else words // E ** 3
                            sp.dma_start(WUP[:, u, a, :],
                                         up_weights[ds(e, 1), :, :].rearrange("o d h -> (o d) h")).then_inc(up_in[u], 16)

                def rows(d, v):
                    sp.dma_start(xs[:, v, :, :],
                                 rows_in[g][ds(d * 4 * P, 4 * P), :].rearrange("(q p) d -> p q d", p=P)).then_inc(xs_in[v], 16)

                sp.wait_ge(rows_ready, rn + 1)
                load_weights(0, 0, n > 0)
                sp.wait_ge(scattered[rn % XBUF], 16 * 2 * T * (rn // XBUF + 1))
                for d in range(2):
                    load_rows(d, n > 0)
                    rows(d, d)
                load_weights(1, 1, n > 0)
                with sp.Fori(1, NP // SLOTS) as q:
                    for v in range(2):
                        load_rows(q * 2 + v)
                        rows(q * 2 + v, v)
                        load_weights(q * 2 + v, v)

            waiting = []
            for st in ORDER:
                if st[0] == "E":
                    experts(kind_no[st], st[1], st[2])
                    for cn, g in waiting:
                        sp.wait_ge(combined, T * (cn + 1))
                        sp.dma_start(out_v[g], X[:, g, :, :]).then_inc(stored, 16)
                    waiting = []
                if st[0] == "C" and st[1] == 1:
                    waiting.append((kind_no[st], st[2]))
            for cn, g in waiting:
                sp.wait_ge(combined, T * (cn + 1))
                sp.dma_start(out_v[g], X[:, g, :, :]).then_inc(stored, 16)
            sp.wait_ge(stored, 16 * G)
            for u in range(2):
                sp.wait_ge(eo_out[u], 16 * (NP // SLOTS) * 2 * G)

        @block.gpsimd
        def _(pool):
            chain = [0]

            def link(ins):
                chain[0] += 1
                ins.then_inc(pool_chain, 1)
                pool.wait_ge(pool_chain, chain[0])

            pool.memset(zeros, 0.0).then_inc(zero_ready, 1)
            pool.memset(ones[:], 1.0)
            link(pool.memset(onesf[:], 1.0))
            pool.affine_select(out=ident[:], in_=onesf[:], compare_op=ALU.is_equal, fill=0.0, base=0,
                               pattern=[[-1, P]], channel_multiplier=1)
            pool.affine_select(out=before[:], in_=onesf[:], compare_op=ALU.is_gt, fill=0.0, base=0,
                               pattern=[[1, P]], channel_multiplier=-1)
            link(pool.iota(iota_i[:], [[1, NT]], base=0, channel_multiplier=0))
            link(pool.memset(keep[:], 1.0))
            pool.memset(keep[:, :, 0:1], 0.0)
            pool.tensor_copy(iota_f[:], iota_i[:]).then_inc(consts, 1)

            def scatter(n, f, g):
                pool.wait_ge(rows_ready, n + 1)
                pool.wait_ge(zeroed[g], 16 * (NT // T))
                for j in range(T):
                    for k in range(2):
                        pool.indirect_dma_start(rows_in[g], bass.IndirectOffsetOnAxis(IDX[:, g, j, k:k + 1], 0),
                                                XL[:, n % XBUF, j, :], None).then_inc(scattered[n % XBUF], 16)

            def gather(n, en, f, g):
                for u in range(2):
                    pool.wait_ge(eo_out[u], 16 * (NP // SLOTS) * (en + 1))
                for j in range(T):
                    u = j % RING
                    if n * T + j >= RING:
                        pool.wait_ge(combined, n * T + j - RING + 1)
                    for k in range(2):
                        pool.indirect_dma_start(got[:, u, k, :], None, rows_out[g],
                                                bass.IndirectOffsetOnAxis(IDX[:, g, j, k:k + 1], 0)).then_inc(got_in[u], 16)

            for st in ORDER:
                if st[0] == "K":
                    scatter(kind_no[st], st[1], st[2])
                if st[0] == "G":
                    gather(kind_no[st], kind_no[("E",) + st[1:]], st[1], st[2])

        @block.scalar
        def _(act):
            def normalize(n, g, out, col, ready):
                for i in range(4):
                    for j in range(4 * i, 4 * i + 4):
                        ins = act.activation(out[:, j, :], X[:, g, j, :], ACT.Identity,
                                             scale=rs[:, col + j:col + j + 1], bias=nb[:, col + j:col + j + 1])
                    ins.then_inc(ready, 1)

            def norm(n, router, ga):
                act.wait_ge(norm_ready, n + 1)
                if router is not None:
                    rn = kind_no[("R",) + router]
                    if rn >= XBUF:
                        act.wait_ge(scattered[rn % XBUF], 16 * 2 * T * (rn // XBUF))
                    normalize(n, router[1], XL[:, rn % XBUF, :, :], 0, xl_ready)
                if ga is not None:
                    normalize(n, ga, XN, T, xn_ready)

            def route(n):
                for i in range(4):
                    act.wait_ge(xt_ps, 4 * n + i + 1)
                    act.activation(XT[:, i * 512:(i + 1) * 512], ps[i][:], ACT.Copy).then_inc(xt_sb, 1)

            def weigh(n):
                act.wait_ge(gap_ready, n + 1)
                act.activation(gexp[:], gap[:], ACT.Exp).then_inc(gap_exp, 1)

            def experts(n, g):
                at = n * NP

                def gelu(m, v, u):
                    act.wait_ge(hid_ps, at + m + 1)
                    for k in range(4):
                        ins = act.activation(hidT[:, v, k * P:(k + 1) * P], ps[2 + v][:, k * P:(k + 1) * P], ACT.Gelu,
                                             bias=WUP[:, u, k // 2, H + k % 2:H + k % 2 + 1])
                    ins.then_inc(hid_sb, 1)

                def move_eo(m, u, q=None):
                    act.wait_ge(eo_ps, at + m + 1)
                    if q is not None and u % 2 == 0:
                        act.wait_ge(eo_out[u // 2], 16 * (n * (NP // SLOTS) + q))
                    act.activation(eo[:, u // 2, u % 2 * 2:u % 2 * 2 + 2, :].rearrange("p a b -> p (a b)"),
                                   ps[6 + u % 2][:, 0:256], ACT.Copy).then_inc(eo_sb, 1)

                def store(m, u):
                    act.wait_ge(eo_sb, at + m + 2)
                    act.dma_start(rows_out[g][ds(m * 2 * P, 4 * P), :].rearrange("(q p) d -> p q d", p=P),
                                  eo[:, u // 2, :, :]).then_inc(eo_out[u // 2], 16)

                def move_xsT(m, v):
                    act.wait_ge(xsT_ps, at + m + 1)
                    act.activation(xsT[:, v, :], ps[v][:, 0:256], ACT.Copy).then_inc(xsT_sb, 1)

                def step(m, u, q, static):
                    if not static or m < NP:
                        gelu(m, u % 2, u)
                    if u % 2 == 1 and (not static or m >= 3):
                        store(m - 3, (u - 3) % SLOTS)
                    if not static or m + 2 < NP:
                        move_xsT(m + 2, u % 2)
                    if not static or m >= 1:
                        late = q + (u - 1) // SLOTS
                        move_eo(m - 1, (u - 1) % SLOTS, late if not static or late + n > 0 else None)

                move_xsT(0, 0)
                move_xsT(1, 1)
                for m in range(2 * SLOTS):
                    step(m, m % SLOTS, m // SLOTS, True)
                with act.Fori(2, NP // SLOTS - 1) as q:
                    for u in range(SLOTS):
                        step(q * SLOTS + u, u, q, False)
                for m in range(NP - SLOTS, NP + 1):
                    step(m, m % SLOTS, m // SLOTS, True)
                store(NP - 2, (NP - 2) % SLOTS)

            def attention(n, g, routed):
                act.wait_ge(logits_ps, routed)
                for i in range(4):
                    act.wait_ge(xnT_ps, 4 * n + i + 1)
                    act.activation(XT[:, i * 512:(i + 1) * 512], ps[i][:], ACT.Copy, scale=GS[:, 0:1]).then_inc(xnT_sb, 1)
                for blk in range(4):
                    cols = slice(blk * 512, (blk + 1) * 512)
                    steps = slice(blk * 4, blk * 4 + 4)

                    def bank(w):
                        return ps[(4 + blk * 6 + w) % 8]

                    def there(w):
                        act.wait_ge(proj_ps, 24 * n + 6 * blk + w + 1)

                    there(0)
                    act.activation(qg[:, cols], bank(0)[:], ACT.Copy).then_inc(proj_act, 1)
                    there(1)
                    act.activation(tmp[3][:, cols], bank(1)[:], ACT.Copy).then_inc(proj_act, 1)
                    there(2)
                    act.activation(kv[:, cols], bank(2)[:], ACT.Copy).then_inc(proj_act, 1)
                    there(4)
                    act.activation(cr[:, steps, :].rearrange("p a b -> p (a b)"), bank(4)[:], ACT.Copy)
                    act.activation(tmp[0][:, cols], bank(4)[:], ACT.Square).then_inc(proj_act, 1)
                    there(5)
                    act.activation(ci[:, steps, :].rearrange("p a b -> p (a b)"), bank(5)[:], ACT.Copy)
                    act.activation(tmp[1][:, cols], bank(5)[:], ACT.Square).then_inc(proj_act, 1)
                act.wait_ge(r2_ready, n + 1)
                act.activation(tmp[2], tmp[0], ACT.Sqrt).then_inc(r_ready, 1)

            def gate(n):
                act.wait_ge(r_ready, n + 1)
                act.activation(tmp[0], tmp[2], ACT.Ln).then_inc(log_ready, 1)
                act.wait_ge(log_ready, n + 1)
                act.activation(tmp[0], tmp[0], ACT.Exp, scale=-1.0).then_inc(inv_ready, 1)
                act.activation(tmp[1], tmp[2], ACT.Sigmoid).then_inc(m_ready, 1)
                act.activation(tmp[3], tmp[3], ACT.Silu).then_inc(sg_ready, 1)

            act.wait_ge(w_in, small_weights)
            act.activation(GS[:], GM[:], ACT.Copy, scale=float(D) ** 0.5).then_inc(gs_ready, 1)
            act.wait_ge(gs_ready, 1)
            routed = 0
            for st in ORDER:
                if st[0] == "N":
                    norm(kind_no[st], st[1], st[2])
                if st[0] == "R":
                    route(kind_no[st])
                    routed += 1
                if st[0] == "K":
                    weigh(kind_no[st])
                if st[0] == "E":
                    experts(kind_no[st], st[2])
                if st[0] == "A":
                    attention(kind_no[st], st[1], routed)
                if st[0] == "A1":
                    gate(kind_no[st])

        @block.tensor
        def _(pe):
            def free_banks(st):
                old = psum_before[st]
                if old is None:
                    return
                done = kind_no[old] + 1
                if old[0] == "R":
                    pe.wait_ge(logits_read, done)
                if old[0] == "K":
                    pe.wait_ge(rank_read, done)
                if old[0] == "E":
                    pe.wait_ge(eo_sb, NP * done)
                if old[0] == "A":
                    pe.wait_ge(proj_act, 20 * done)
                    pe.wait_ge(proj_dve, 4 * done)
                if old[0] == "A3":
                    pe.wait_ge(x_added, 4 * done)

            def route(st, n):
                free_banks(st)
                if n == 0:
                    pe.wait_ge(consts, 1)
                for i in range(4):
                    pe.wait_ge(xl_ready, 4 * n + i + 1)
                    for j in range(4):
                        ins = pe.transpose(ps[i][:, j * P:(j + 1) * P], XL[:, n % XBUF, 4 * i + j, :], ident[:])
                    ins.then_inc(xt_ps, 1)
                if n == 0:
                    pe.wait_ge(w_in, small_weights)
                for j in range(T):
                    if j % 4 == 0:
                        pe.wait_ge(xt_sb, 4 * n + j // 4 + 1)
                    ins = pe.matmul(ps[4][:, j * E:(j + 1) * E], XT[:, j * P:(j + 1) * P], WR[:], start=True, stop=True)
                ins.then_inc(logits_ps, 1)

            def rank(st, n):
                free_banks(st)
                pe.wait_ge(mask_ready, n + 1)
                flat = mask[:].rearrange("p t e -> p (t e)")
                pe.matmul(ps[5][:, 0:T * E], before[:], flat, start=True, stop=True)
                pe.matmul(ps[5][:, T * E:2 * T * E], ones[:], flat, start=True, stop=True).then_inc(rank_ps, 1)

            def experts(st, n, f, g):
                at = n * NP
                free_banks(st)
                pe.wait_ge(rows_ready, kind_no[("R", f, g)] + 1)
                if n == 0:
                    pe.wait_ge(bias_rows, 16)
                    pe.wait_ge(down_in, down_weights)

                def turn_x(m, u, q):
                    if u % 2 == 0:
                        pe.wait_ge(xs_in[u // 2], 16 * (n * (NP // SLOTS) + q + 1))
                    for a in range(2):
                        ins = pe.transpose(ps[u % 2][:, a * P:(a + 1) * P], xs[:, u // 2, u % 2 * 2 + a, :], ident[:])
                    ins.then_inc(xsT_ps, 1)

                def up(m, u, q):
                    pe.wait_ge(up_in[u], 32 * (n * (NP // SLOTS) + q + 1))
                    pe.wait_ge(xsT_sb, at + m + 1)
                    for a in range(2):
                        for c in range(2):
                            k = 2 * a + c
                            ins = pe.matmul(ps[2 + u % 2][:, k * P:(k + 1) * P], WUP[:, u, a, c * P:(c + 1) * P],
                                            xsT[:, u % 2, a * P:(a + 1) * P], start=True, stop=True)
                    ins.then_inc(hid_ps, 1)

                def experts_of(m):
                    both = pe.value_load(TE2[0:1, g, ds(m, 1)], min_val=0, max_val=E * E - 1)
                    return both % E, both // E

                def down(m, v, pair, old):
                    pe.wait_ge(hid_sb, at + m + 1)
                    if old:
                        pe.wait_ge(eo_sb, at + m - 1)
                    for a, e in enumerate(pair):
                        o = ps[6 + v][:, a * D:(a + 1) * D]
                        for c in range(2):
                            pe.matmul(o, hidT[:, v, (2 * a + c) * P:(2 * a + c + 1) * P],
                                      W2[:, ds(e * H + c * D, D)], start=(c == 0), stop=False)
                        ins = pe.matmul(o, ones[0:3, :], B2R[:, ds(e * D, D)], start=False, stop=True)
                    ins.then_inc(eo_ps, 1)

                def step(m, u, q, static):
                    if not static or m < NP:
                        up(m, u, q)
                    if not static or m >= 1:
                        pair = experts_of(m - 1)
                    if not static or m + 2 < NP:
                        turn_x(m + 2, (u + 2) % SLOTS, q + (u + 2) // SLOTS)
                    if not static or m >= 1:
                        down(m - 1, (u - 1) % 2, pair, not static or m >= 3)

                turn_x(0, 0, 0)
                turn_x(1, 1, 0)
                for m in range(SLOTS):
                    step(m, m, 0, True)
                with pe.Fori(1, NP // SLOTS - 1) as q:
                    for u in range(SLOTS):
                        step(q * SLOTS + u, u, q, False)
                for m in range(NP - SLOTS, NP + 1):
                    step(m, m % SLOTS, m // SLOTS, True)

            def attention(st, n, g):
                free_banks(st)
                for i in range(4):
                    pe.wait_ge(xn_ready, 4 * n + i + 1)
                    for j in range(4):
                        ins = pe.transpose(ps[i][:, j * P:(j + 1) * P], XN[:, 4 * i + j, :], ident[:])
                    ins.then_inc(xnT_ps, 1)
                for blk in range(4):
                    pe.wait_ge(xnT_sb, 4 * n + blk + 1)
                    for w in range(6):
                        k = blk * 6 + w
                        if 4 + k - 8 >= 0 and k < 8:
                            pe.wait_ge(xnT_sb, 4 * n + min(k - 3, 4))
                        if k >= 8:
                            old = k - 8
                            if old % 6 == 3:
                                pe.wait_ge(proj_dve, 4 * n + old // 6 + 1)
                            else:
                                pe.wait_ge(proj_act, 20 * n + 5 * (old // 6) + [1, 2, 3, 0, 4, 5][old % 6])
                        pe.matmul(ps[(4 + k) % 8][:], WA[:, w, :], XT[:, blk * 512:(blk + 1) * 512],
                                  start=True, stop=True).then_inc(proj_ps, 1)

            def project(st, n, g):
                free_banks(st)
                pe.wait_ge(y_ready, n + 1)
                for i in range(4):
                    for j in range(4):
                        ins = pe.matmul(ps[i][:, j * D:(j + 1) * D], kv[:, (4 * i + j) * P:(4 * i + j + 1) * P], WO[:],
                                        start=True, stop=True)
                    ins.then_inc(wo_ps, 1)

            for st in ORDER:
                if st[0] == "R":
                    route(st, kind_no[st])
                if st[0] == "K":
                    rank(st, kind_no[st])
                if st[0] == "E":
                    experts(st, kind_no[st], st[1], st[2])
                if st[0] == "A":
                    attention(st, kind_no[st], st[1])
                if st[0] == "A3":
                    project(st, kind_no[st], st[1])

        @block.vector
        def _(dve):
            chain = [0]

            def link(ins, times=1):
                chain[0] += times
                ins.then_inc(dve_chain, 1)
                dve.wait_ge(dve_chain, chain[0])

            def norm(n, router, ga):
                if router is not None and router[0] == 0:
                    dve.wait_ge(x_in[router[1]], 16)
                if ga == 0:
                    for i in range(G):
                        dve.wait_ge(zeroed[i], 16 * (NT // T))
                for g, col in ((router and router[1], 0), (ga, T)):
                    if g is None:
                        continue
                    with dve.Fori(0, T // 4) as i:
                        for u in range(4):
                            ins = dve.bn_stats(stats[:, ds(i * 4 + (u + col), 1), :].rearrange("p a b -> p (a b)"),
                                               X[:, g, ds(i * 4 + u, 1), :].rearrange("p a b -> p (a b)"))
                        ins.then_inc(dve_chain, 1)
                    chain[0] += T // 4
                c = slice(0 if router else T, T if ga is None else 2 * T)
                dve.wait_ge(dve_chain, chain[0])
                dve.tensor_tensor(m2[:, c], stats[:, c, 1], stats[:, c, 4], add)
                dve.tensor_tensor(df[:, c], stats[:, c, 1], stats[:, c, 4], sub)
                link(dve.tensor_tensor(var[:, c], stats[:, c, 2], stats[:, c, 5], add))
                link(dve.scalar_tensor_tensor(out=df[:, c], in0=df[:, c], scalar=0.25, in1=df[:, c], op0=mult, op1=mult))
                link(dve.scalar_tensor_tensor(out=var[:, c], in0=var[:, c], scalar=1.0 / D, in1=df[:, c], op0=mult, op1=add))
                if router is not None:
                    ins = dve.tensor_scalar(var[:, 0:T], var[:, 0:T], EPS, None, add)
                if ga is not None:
                    ins = dve.tensor_scalar(var[:, T:2 * T], var[:, T:2 * T], float(D) + EPS, EPS * EPS, mult, add)
                link(ins)
                dve.tensor_scalar(vh[:, c], var[:, c], -0.5, None, mult)
                link(dve.tensor_scalar(seed[:, c], var[:, c].bitcast(u32), 1, None, ALU.logical_shift_right))
                link(dve.tensor_scalar(rs[:, c].bitcast(i32), seed[:, c], -1.0, float(0x5f3759df), mult, add))
                for _ in range(3):
                    link(dve.tensor_tensor(na[:, c], rs[:, c], rs[:, c], mult))
                    link(dve.tensor_tensor(na[:, c], na[:, c], vh[:, c], mult))
                    link(dve.scalar_tensor_tensor(out=rs[:, c], in0=na[:, c], scalar=1.5, in1=rs[:, c], op0=add, op1=mult))
                dve.scalar_tensor_tensor(out=nb[:, c], in0=m2[:, c], scalar=-0.5, in1=rs[:, c],
                                         op0=mult, op1=mult).then_inc(norm_ready, 1)

            def route(n, f, g):
                xl = XL[:, n % XBUF, :, :]
                dve.wait_ge(xl_ready, (T // 4) * (n + 1))
                xg = X[:, g, :, :].rearrange("p t d -> p (t d)")
                dve.scalar_tensor_tensor(out=xg, in0=xl.rearrange("p t d -> p (t d)"), scalar=0.5, in1=xg, op0=mult, op1=add)
                dve.wait_ge(logits_ps, n + 1)
                dve.tensor_tensor(LG[:], ps[4][:, 0:T * E].rearrange("p (t e) -> p t e", t=T),
                                  BR[:].unsqueeze(1).broadcast_to([P, T, E]), add).then_inc(logits_read, 1)
                dve.wait_ge(logits_read, n + 1)
                for j in range(T):
                    ins = dve.max(MX[:, j, :], LG[:, j, :])
                link(ins)
                dve.tensor_tensor(gap[:], MX[:, :, 1], MX[:, :, 0], sub).then_inc(gap_ready, 1)
                for j in range(T):
                    ins = dve.max_index(IX[:, j, :], MX[:, j, :], LG[:, j, :])
                link(ins)
                link(dve.tensor_copy(IXF[:], IX[:, :, 0:2]))
                for k in range(2):
                    ins = dve.tensor_tensor(hot[:, k, :, :], iota_f[:, 0:E].unsqueeze(1).broadcast_to([P, T, E]),
                                            IXF[:, :, k:k + 1].broadcast_to([P, T, E]), ALU.is_equal)
                link(ins)
                dve.tensor_tensor(mask[:], hot[:, 0, :, :], hot[:, 1, :, :], add).then_inc(mask_ready, 1)

            def rank(n, f, g):
                link(dve.memset(cnt[:, :, 0:1], 0.0))
                dve.wait_ge(rank_ps, n + 1)
                link(dve.tensor_copy(cnt[:, :, 1:T + 1], ps[5][:, T * E:2 * T * E].rearrange("p (t e) -> p e t", t=T)))
                link(dve.tensor_tensor_scan(off[:].rearrange("p e t -> p (e t)"), keep[:].rearrange("p e t -> p (e t)"),
                                            cnt[:].rearrange("p e t -> p (e t)"), 0.0, mult, add))
                link(dve.tensor_scalar(nte[:], off[:, :, T:T + 1].rearrange("p e o -> p (e o)"), 1.0 / P, 127.0 / 256.0, mult, add))
                link(dve.tensor_scalar(nte[:], nte[:], 12582912.0, -12582912.0, add, add))
                link(dve.tensor_tensor_scan(cum[:], onesf[:, 0:E], nte[:], 0.0, mult, add))
                link(dve.tensor_tensor(basee[:], cum[:], nte[:], sub))
                link(dve.scalar_tensor_tensor(out=off[:, :, 0:T], in0=basee[:].unsqueeze(2).broadcast_to([P, E, T]),
                                              scalar=float(P), in1=off[:, :, 0:T], op0=mult, op1=add))
                ins = dve.tensor_tensor(pos[:], ps[5][:, 0:T * E].rearrange("p (t e) -> p t e", t=T),
                                        off[:, :, 0:T].rearrange("p e t -> p t e"), add)
                ins.then_inc(rank_read, 1)
                dve.wait_ge(rank_read, n + 1)
                for k in range(2):
                    ins = dve.tensor_tensor(sel[:, k, :, :], hot[:, k, :, :], pos[:], mult)
                link(ins)
                for k in range(2):
                    ins = dve.tensor_reduce(rowf[:, :, k:k + 1], sel[:, k, :, :], AX.X, add)
                link(ins)
                dve.tensor_copy(IDX[:, g, :, :], rowf[:])
                link(dve.tensor_tensor(tcmp, iota_f[0:1, :].unsqueeze(2).broadcast_to([1, NT, E]),
                                       cum[0:1, :].unsqueeze(1).broadcast_to([1, NT, E]), ALU.is_ge))
                link(dve.tensor_reduce(tef[:].unsqueeze(2), tcmp, AX.X, add))
                link(dve.tensor_scalar(tef[:], tef[:], float(E - 1), None, ALU.min))
                tef2, tep2 = tef[:].rearrange("o (i a) -> o i a", a=2), tep[:].rearrange("o (i a) -> o i a", a=2)
                link(dve.scalar_tensor_tensor(out=tep[:], in0=tef2[:, :, 1], scalar=float(E), in1=tef2[:, :, 0],
                                              op0=mult, op1=add))
                dve.tensor_copy(TE2[0:1, g, :], tep[:])
                dve.scalar_tensor_tensor(out=TE4[0:1, g, :], in0=tep2[:, :, 1], scalar=float(E * E), in1=tep2[:, :, 0],
                                         op0=mult, op1=add).then_inc(rows_ready, 1)
                dve.wait_ge(gap_exp, n + 1)
                link(dve.tensor_scalar(den[:], gexp[:], 1.0, None, add))
                link(dve.reciprocal(den[:], den[:]))
                link(dve.tensor_scalar(WGT[:, g, 0, :], den[:], 0.5, None, mult))
                link(dve.tensor_tensor(WGT[:, g, 1, :], WGT[:, g, 0, :], gexp[:], mult))

            def combine(n, g):
                with dve.Fori(0, T // RING) as q:
                    for half in range(2):
                        for u in range(half * 4, half * 4 + 4):
                            dve.wait_ge(got_in[u], q * 32 + 32 * (n * (T // RING) + 1))
                        for k in range(2):
                            for u in range(half * 4, half * 4 + 4):
                                j = ds(q * RING + u, 1)
                                xt = X[:, g, j, :].rearrange("p a b -> p (a b)")
                                ins = dve.scalar_tensor_tensor(out=xt, in0=got[:, u, k, :], scalar=WGT[:, g, k, j], in1=xt,
                                                               op0=mult, op1=add)
                                if k == 1:
                                    ins.then_inc(combined, 1)
                            if k == 0:
                                ins.then_inc(dve_chain, 1)
                                dve.wait_ge(dve_chain, q * 2 + (chain[0] + 1 + half))
                chain[0] += 2 * (T // RING)
                dve.wait_ge(combined, T * (n + 1))

            def attention(n, g):
                for blk in range(4):
                    cols = slice(blk * 512, (blk + 1) * 512)
                    dve.wait_ge(proj_act, 20 * n + 5 * blk + 3)
                    dve.wait_ge(proj_ps, 24 * n + 6 * blk + 4)
                    dve.tensor_tensor(kv[:, cols], ps[(4 + blk * 6 + 3) % 8][:], kv[:, cols], mult).then_inc(proj_dve, 1)
                dve.wait_ge(proj_act, 20 * (n + 1))
                dve.scalar_tensor_tensor(out=tmp[0], in0=tmp[0], scalar=TINY * TINY, in1=tmp[1],
                                         op0=add, op1=add).then_inc(r2_ready, 1)

            def gate(n):
                crf, cif = cr[:].rearrange("p l c -> p (l c)"), ci[:].rearrange("p l c -> p (l c)")
                dve.wait_ge(inv_ready, n + 1)
                link(dve.tensor_tensor(XT[:], tmp[2], tmp[0], mult))
                link(dve.scalar_tensor_tensor(out=tmp[0], in0=XT[:], scalar=2.0, in1=tmp[0], op0=sub, op1=mult))
                dve.wait_ge(m_ready, n + 1)
                link(dve.scalar_tensor_tensor(out=tmp[0], in0=tmp[0], scalar=-1.0, in1=tmp[1], op0=mult, op1=mult))
                dve.scalar_tensor_tensor(out=crf, in0=crf, scalar=TINY, in1=tmp[0], op0=add, op1=mult)
                dve.tensor_tensor(cif, cif, tmp[0], mult)
                dve.wait_ge(sg_ready, n + 1)
                link(dve.tensor_tensor(qg[:], qg[:], tmp[3], mult))

            def scan(n):
                dve.tensor_copy(S[:, 0, 0, :], kv[:, 0:P])
                dve.memset(S[:, 0, 1, :], 0.0)
                dve.tensor_copy(S[:, 0, 2, :], cr[:, 0, :])
                link(dve.tensor_copy(S[:, 0, 3, :], ci[:, 0, :]))
                base = chain[0] - 5
                with dve.Fori(1, T) as l:
                    old = S[:, ds(l - 1, 1), :, :].rearrange("p o f c -> p (o f) c")
                    new = S[:, ds(l, 1), :, :].rearrange("p o f c -> p (o f) c")
                    hr = S[:, ds(l, 1), 0, :].rearrange("p o c -> p (o c)")
                    ar, ai = (t[:, ds(l, 1), :].broadcast_to([P, 2, P]) for t in (cr, ci))

                    def done(k):
                        dve.wait_ge(dve_chain, l * 5 + (base + k))

                    done(3 - 5)
                    dve.tensor_tensor(t1[:, 2:4, :], ar, old[:, 2:4, :], mult)
                    dve.tensor_tensor(t2[:, 2:4, :], ai, old[:, 2:4, :], mult).then_inc(dve_chain, 1)
                    done(5 - 5)
                    dve.tensor_tensor(t1[:, 0:2, :], ar, old[:, 0:2, :], mult)
                    dve.tensor_tensor(t2[:, 0:2, :], ai, old[:, 0:2, :], mult).then_inc(dve_chain, 1)
                    done(1)
                    dve.tensor_tensor(new[:, 2, :], t1[:, 2, :], t2[:, 3, :], sub)
                    dve.tensor_tensor(new[:, 3, :], t1[:, 3, :], t2[:, 2, :], add).then_inc(dve_chain, 1)
                    done(2)
                    dve.tensor_tensor(new[:, 0, :], t1[:, 0, :], t2[:, 1, :], sub).then_inc(dve_chain, 1)
                    dve.tensor_tensor(new[:, 1, :], t1[:, 1, :], t2[:, 0, :], add)
                    done(4)
                    dve.tensor_tensor(hr, hr, kv[:, ds(l * P, P)], add).then_inc(dve_chain, 1)
                chain[0] += 5 * (T - 1)
                dve.wait_ge(dve_chain, chain[0])
                link(dve.tensor_copy(Y[:], S[:, T - 1, :, :].rearrange("p f (b c) -> p f b c", b=BG)))
                d = 1
                while d < C:
                    m = C - d
                    rows = 4 if 2 * d < C else 2
                    p1, p2 = (t[:, 0:rows, 0:BG * m].rearrange("p f (b c) -> p f b c", b=BG) for t in (t1, t2))
                    for p, f in ((p1, 2), (p2, 3)):
                        ins = dve.tensor_tensor(p, Y[:, f:f + 1, :, d:C].broadcast_to([P, rows, BG, m]),
                                                Y[:, 0:rows, :, 0:m], mult)
                    link(ins)
                    for f in range(0, rows, 2):
                        dve.tensor_tensor(p1[:, f, :, :], p1[:, f, :, :], p2[:, f + 1, :, :], sub)
                        ins = dve.tensor_tensor(p1[:, f + 1, :, :], p1[:, f + 1, :, :], p2[:, f, :, :], add)
                    link(ins)
                    ins = dve.tensor_tensor(Y[:, 0:2, :, d:C], Y[:, 0:2, :, d:C], p1[:, 0:2, :, :], add)
                    if rows == 4:
                        ins = dve.tensor_copy(Y[:, 2:4, :, d:C], p1[:, 2:4, :, :])
                    link(ins)
                    d *= 2
                h, ar, ai = (S[:, :, f, :].rearrange("p l (b c) -> p l b c", b=BG)[:, :, :, 1:C] for f in (0, 2, 3))
                kr, ki = (Y[:, f:f + 1, :, 0:C - 1].broadcast_to([P, T, BG, C - 1]) for f in (0, 1))
                dve.tensor_tensor(ar, ar, kr, mult)
                link(dve.tensor_tensor(ai, ai, ki, mult))
                link(dve.tensor_tensor(h, h, ar, add))
                link(dve.tensor_tensor(h, h, ai, sub))
                dve.tensor_tensor(kv[:].rearrange("p (l c) -> p l c", l=T), S[:, :, 0, :],
                                  qg[:].rearrange("p (l c) -> p l c", l=T), mult).then_inc(y_ready, 1)

            def add_attention(n, g):
                for i in range(4):
                    dve.wait_ge(wo_ps, 4 * n + i + 1)
                    xq = X[:, g, 4 * i:4 * i + 4, :].rearrange("p t d -> p (t d)")
                    dve.tensor_tensor(xq, ps[i][:], xq, add).then_inc(x_added, 1)
                dve.wait_ge(x_added, 4 * (n + 1))

            dve.wait_ge(bias_in, 16)
            for k in range(2):
                link(dve.tensor_copy(b2p[:, k, :], b2f))
                link(dve.tensor_tensor(b2f, b2f, b2p[:, k, :], sub))
            dve.tensor_copy(b2p[:, 2, :], b2f).then_inc(parts_ready, 1)
            dve.wait_ge(consts, 1)
            dve.wait_ge(w_in, small_weights)
            for st in ORDER:
                if st[0] == "N":
                    norm(kind_no[st], st[1], st[2])
                if st[0] == "R":
                    route(kind_no[st], st[1], st[2])
                if st[0] == "K":
                    rank(kind_no[st], st[1], st[2])
                if st[0] == "C":
                    combine(kind_no[st], st[2])
                if st[0] == "A":
                    attention(kind_no[st], st[1])
                if st[0] == "A1":
                    gate(kind_no[st])
                if st[0] == "A2":
                    scan(kind_no[st])
                if st[0] == "A3":
                    add_attention(kind_no[st], st[1])


_INS = ["L0_attn_x", "L0_attn_gamma", "L0_attn_wq", "L0_attn_wk", "L0_attn_wv", "L0_attn_wa", "L0_attn_wg", "L0_attn_wo",
        "L0_ffn_Wr", "L0_ffn_br", "L0_ffn_W1", "L0_ffn_b1", "L0_ffn_W2", "L0_ffn_b2"]


def kernel(**inputs):
    import numpy as np
    import concourse.bacc as bacc
    from concourse.bass_utils import run_bass_kernel_spmd as run

    nc = bacc.Bacc("TRN2", target_bir_lowering=False, num_devices=1)
    arrays, args = {}, []
    for name in _INS:
        a = np.ascontiguousarray(inputs[name])
        arrays["in_" + name] = a
        args.append(nc.dram_tensor("in_" + name, a.shape, mybir.dt.from_np(a.dtype), kind="ExternalInput").ap())
    args.append(nc.dram_tensor("out_0", (B, N, D), mybir.dt.float32, kind="ExternalOutput").ap())
    build(nc, *args)
    return run(nc, [arrays], core_ids=[0]).results[0]["out_0"]
```

```python
import concourse.bass as bass
from concourse import mybir
from contextlib import ExitStack

P = 128
D = 128
B, N = 32, 256
E, H = 16, 256
G = 4
T = B * N // G // P
C = N // T
BG = B // G
NT = 2 * T + E
NP = NT // 2
SLOTS = 4
XBUF = 3
EPS = 1e-5
TINY = 1e-18

ORDER = [("N", (0, 0), None), ("R", 0, 0), ("K", 0, 0, 0), ("W", 0, 0), ("N", (0, 1), None), ("R", 0, 1), ("K", 0, 1, 0),
         ("W", 0, 1), ("N", (0, 2), None), ("N", (0, 3), None), ("E", 0, 0, 0, 0, 24), ("R", 0, 2), ("G", 0, 0, 0, 4),
         ("K", 0, 2, 0), ("W", 0, 2), ("R", 0, 3), ("E", 0, 1, 0, 0, 12), ("C", 0, 0, 0, 4), ("S", 0), ("N", None, 0),
         ("T", 0), ("A0", 0), ("K", 0, 3, 0), ("A", 0), ("I", 0), ("W", 0, 3), ("A1", 0), ("G", 0, 1, 0, 4),
         ("E", 0, 1, 0, 12, 24), ("E", 0, 2, 0, 0, 12), ("A2", 0), ("A3", 0), ("C", 0, 1, 0, 4), ("S", 1),
         ("E", 0, 2, 0, 12, 24), ("N", (1, 0), 1), ("R", 1, 0), ("T", 1), ("A0", 1), ("G", 0, 2, 0, 4), ("K", 1, 0, 0),
         ("A", 1), ("C", 0, 2, 0, 3), ("I", 1), ("W", 1, 0), ("A1", 1), ("E", 0, 3, 0, 0, 24),
         ("A2", 1), ("C", 0, 2, 3, 4), ("S", 2), ("A3", 1), ("G", 0, 3, 0, 2),
         ("E", 1, 0, 0, 0, 4), ("N", (1, 1), 2), ("R", 1, 1), ("T", 2), ("A0", 2), ("G", 0, 3, 2, 4), ("K", 1, 1, 0),
         ("A", 2), ("C", 0, 3, 0, 4), ("I", 2), ("W", 1, 1), ("A1", 2), ("E", 1, 0, 0, 4, 24), ("E", 1, 1, 0, 0, 4),
         ("A2", 2), ("S", 3), ("A3", 2), ("G", 1, 0, 0, 2),
         ("E", 1, 1, 0, 4, 8), ("N", (1, 2), 3), ("R", 1, 2), ("T", 3), ("A0", 3), ("G", 1, 0, 2, 4), ("K", 1, 2, 0),
         ("A", 3), ("C", 1, 0, 0, 4), ("I", 3), ("W", 1, 2), ("A1", 3), ("E", 1, 1, 0, 8, 24), ("E", 1, 2, 0, 0, 8),
         ("A2", 3), ("A3", 3),
         ("E", 1, 2, 0, 8, 12), ("N", (1, 3), None), ("R", 1, 3), ("G", 1, 1, 0, 4), ("K", 1, 3, 0), ("K", 1, 3, 1), ("W", 1, 3),
         ("C", 1, 1, 0, 4), ("E", 1, 2, 0, 12, 24), ("E", 1, 3, 0, 0, 20), ("G", 1, 2, 0, 4),
         ("C", 1, 2, 0, 4), ("E", 1, 3, 1, 0, 12), ("G", 1, 3, 0, 3), ("C", 1, 3, 0, 3), ("G", 1, 3, 3, 4),
         ("C", 1, 3, 3, 4)]
HALVED = ((1, 3),)
SLOT = {(f, g, 0): g for f in range(2) for g in range(G)}
SLOT.update({(f, g, 1): (g + 1) % G for f, g in HALVED})
TILES = {(f, g, h): (T * 3 // 4, T // 4)[h] if (f, g) in HALVED else T for f, g, h in SLOT}


def build(nc, x, gamma, wq, wk, wv, wa, wg, wo, wr, br, w1, b1, w2, b2, out):
    f32, bf16, i32, u32 = mybir.dt.float32, mybir.dt.bfloat16, mybir.dt.int32, mybir.dt.uint32
    ALU = mybir.AluOpType
    ACT = mybir.ActivationFunctionType
    AX = mybir.AxisListType
    ds = bass.ds
    add, sub, mult = ALU.add, ALU.subtract, ALU.mult

    x_v = x.rearrange("(g b) (c l) d -> g (b c) l d", g=G, l=T)
    out_v = out.rearrange("(g b) (c l) d -> g (b c) l d", g=G, l=T)
    rows_in = [nc.dram_tensor(f"rows_in{i}", (NT * P, D), f32, kind="Internal").ap() for i in range(G)]
    rows_out = [nc.dram_tensor(f"rows_out{i}", (NT * P, D), f32, kind="Internal").ap() for i in range(G)]
    up_weights = nc.dram_tensor("up_weights", (E, D, H + 2), f32, kind="Internal").ap()
    bias2_parts = nc.dram_tensor("bias2_parts", (3, E, D), bf16, kind="Internal").ap()

    kind_no = {}
    psum_before = {}
    pairs_by = {}
    pairs_at = {}
    ranks_by = {}
    gathers = []
    seen, last, pairs = {}, None, 0
    for st in ORDER:
        if st[0] == "E":
            pairs_at[st] = pairs
            pairs += st[5] - st[4]
            pairs_by[st[1:4]] = pairs
        if st[0] == "G" and st[1:3] not in gathers:
            gathers.append(st[1:3])
        ranks_by[st] = seen.get("K", 0)
        kind_no[st] = seen.get(st[0], 0)
        seen[st[0]] = kind_no[st] + 1
        psum_before[st] = last
        if st[0] in ("R", "T", "A", "E", "A3"):
            last = st

    def rows_put(f, g, half):
        if half == 1:
            return XBUF + HALVED.index((f, g)), 16 * 2 * TILES[f, g, 1]
        rn = kind_no[("R", f, g)]
        return rn % XBUF, 16 * 2 * sum(TILES[st[1], st[2], 0] for st in kind_no if st[0] == "R"
                                       and kind_no[st] <= rn and kind_no[st] % XBUF == rn % XBUF)

    with ExitStack() as ctx:
        def sb(name, shape, dt):
            return ctx.enter_context(nc.sbuf_tensor(name, shape, dt))

        def sem(name):
            return ctx.enter_context(nc.semaphore(name))

        X = sb("X", [P, G, T, D], f32)
        XL = sb("XL", [P, XBUF, T, D], f32)
        WUP = sb("WUP", [P, SLOTS, 2, H + 2], f32)
        W2 = sb("W2", [P, E * H], f32)
        B2R = sb("B2R", [3, E * D], bf16)
        WA = sb("WA", [P, 6, D], f32)
        WO = sb("WO", [P, D], f32)
        WR = sb("WR", [P, E], f32)
        BR = sb("BR", [P, E], f32)
        GM = sb("GM", [P, 1], f32)
        GS = sb("GS", [P, 1], f32)
        ident = sb("ident", [P, P], f32)
        onesf = sb("onesf", [P, P], f32)
        before = sb("before", [P, P], bf16)
        ones = sb("ones", [P, P], bf16)
        iota_i = sb("iota_i", [P, NT], i32)
        iota_f = sb("iota_f", [P, NT], f32)
        keep = sb("keep", [P, E, T + 1], f32)
        IDX = sb("IDX", [P, G, T, 2], u32)
        WGT = sb("WGT", [P, G, 2, T], f32)
        TE2 = sb("TE2", [1, G, NP], i32)
        TE4 = sb("TE4", [1, G, NP // 2], i32)
        stats = sb("stats", [P, 2 * T, 6], f32)
        m2 = sb("m2", [P, 2 * T], f32)
        df = sb("df", [P, 2 * T], f32)
        var = sb("var", [P, 2 * T], f32)
        vh = sb("vh", [P, 2 * T], f32)
        rs = sb("rs", [P, 2 * T], f32)
        na = sb("na", [P, 2 * T], f32)
        nb = sb("nb", [P, 2 * T], f32)
        XT = sb("XT", [P, T * D], f32)
        LG = sb("LG", [P, T, E], f32)
        MX = sb("MX", [P, T, 8], f32)
        IX = sb("IX", [P, T, 8], u32)
        IXF = sb("IXF", [P, T, 2], f32)
        gap = sb("gap", [P, T], f32)
        gexp = sb("gexp", [P, T], f32)
        den = sb("den", [P, T], f32)
        mask = sb("mask", [P, T, E], bf16)
        cnt = sb("cnt", [P, E, T + 1], f32)
        off = sb("off", [P, E, T + 1], f32)
        nte = sb("nte", [P, E], f32)
        cum = sb("cum", [P, E], f32)
        basee = sb("basee", [P, E], f32)
        pos = sb("pos", [P, T, E], f32)
        rowf = sb("rowf", [P, T, 2], f32)
        tef = sb("tef", [1, NT], f32)
        tep = sb("tep", [1, NP], f32)
        xs = sb("xs", [P, 2, 4, D], f32)
        xsT = sb("xsT", [P, 2, 2 * P], f32)
        hidT = sb("hidT", [P, 2, 4 * P], f32)
        eo = sb("eo", [P, 2, 4, D], f32)
        got = sb("got", [P, T, 2, D], f32)
        kv = sb("kv", [P, T * P], f32)
        cr = sb("cr", [P, T, P], f32)
        ci = sb("ci", [P, T, P], f32)
        qg = sb("qg", [P, T * P], f32)
        S = sb("S", [P, 4 * T * P], f32)
        scratch = sb("scratch", [P, 512 + NT * E], f32)
        W = T * P
        tmp = [S[:, i * W:(i + 1) * W] for i in range(4)]
        XN = kv[:].rearrange("p (l d) -> p l d", l=T)
        def spans(buf, rows, count):
            return buf.rearrange("p (f j c) -> p f j c", f=rows, j=count)

        span2, span4 = spans(S[:, 0:2 * W], 4, T // 2), spans(S[:, 2 * W:3 * W], 4, T // 4)
        span8, span16 = spans(scratch[:, 0:1024], 4, T // 8), spans(XT[:, 0:4 * P], 4, 1)
        before2 = spans(S[:, 3 * W:4 * W], 2, T // 2)
        Y = XT[:, 0:4 * P].rearrange("p (f b c) -> p f b c", f=4, b=BG)
        zeros = kv[:]
        b2f = S[0:E, 0:D]
        b2p = S[0:E, 1024:2048].bitcast(bf16)[:, 0:3 * D].rearrange("e (k h) -> e k h", k=3)
        hot = scratch[:, 0:512].rearrange("p (k t e) -> p k t e", k=2, t=T)
        sel = scratch[:, 512:1024].rearrange("p (k t e) -> p k t e", k=2, t=T)
        tcmp = scratch[0:1, 512:512 + NT * E].rearrange("p (t e) -> p t e", t=NT)
        ps = [ctx.enter_context(nc.psum_tensor(f"bank{i}", [P, 512], f32)) for i in range(8)]

        x_in = [sem(f"x_in{g}") for g in range(G)]
        zeroed = [sem(f"zeroed{i}") for i in range(G)]
        w_in, down_in, up_put = sem("w_in"), sem("down_in"), sem("up_put")
        bias_in, parts_out, bias_rows = sem("bias_in"), sem("parts_out"), sem("bias_rows")
        consts, zero_ready, parts_ready = sem("consts"), sem("zero_ready"), sem("parts_ready")
        dve_chain, pool_chain = sem("dve_chain"), sem("pool_chain")
        rank_read, x_added, gs_ready = sem("rank_read"), sem("x_added"), sem("gs_ready")
        xl_ready, xt_ps, xt_sb, logits_ps = sem("xl_ready"), sem("xt_ps"), sem("xt_sb"), sem("logits_ps")
        gap_ready, gap_exp, mask_ready, rank_ps, rows_ready = (sem("gap_ready"), sem("gap_exp"), sem("mask_ready"),
                                                             sem("rank_ps"), sem("rows_ready"))
        experts_ready = sem("experts_ready")
        scattered = [sem(f"scattered{i}") for i in range(XBUF + len(HALVED))]
        logits_read = sem("logits_read")
        norm_ready, xn_ready_act = sem("norm_ready"), sem("xn_ready_act")
        qg_ready = sem("qg_ready")
        xs_in = [sem(f"xs_in{i}") for i in range(2)]
        eo_out = [sem(f"eo_out{i}") for i in range(2)]
        up_in = [sem(f"up_in{i}") for i in range(SLOTS)]
        xsT_ps, xsT_sb, hid_ps, hid_sb = sem("xsT_ps"), sem("xsT_sb"), sem("hid_ps"), sem("hid_sb")
        eo_ps, eo_sb = sem("eo_ps"), sem("eo_sb")
        got_in = [sem(f"got_in{i}") for i in range(4)]
        combined = sem("combined")
        xn_ready, xnT_ps, xnT_sb = sem("xn_ready"), sem("xnT_ps"), sem("xnT_sb")
        proj_ps, proj_act, proj_dve = sem("proj_ps"), sem("proj_act"), sem("proj_dve")
        r2_ready, r_ready, log_ready, inv_ready = sem("r2_ready"), sem("r_ready"), sem("log_ready"), sem("inv_ready")
        m_ready = sem("m_ready")
        y_ready, wo_ps, stored = sem("y_ready"), sem("wo_ps"), sem("stored")

        block = ctx.enter_context(nc.Block())
        small_weights, down_weights, up_parts = 9 * 16, 2 * 16, 3 * 16

        @block.sync
        def _(sp):
            sp.dma_start(X[:, 0, :, :], x_v[0]).then_inc(x_in[0], 16)
            sp.dma_start(b2f, b2).then_inc(bias_in, 16)
            sp.dma_start(WR[:], wr).then_inc(w_in, 16)
            sp.dma_start(BR[:], br.partition_broadcast(P)).then_inc(w_in, 16)
            sp.dma_start(GM[:], gamma.rearrange("(d o) -> d o", o=1)).then_inc(w_in, 16)
            for i, w in enumerate((wq, wg, wk, wv)):
                sp.dma_start(WA[:, i, :], w).then_inc(w_in, 16)
            sp.dma_start(WA[:, 4:6, :], wa.rearrange("d (a c) -> d a c", a=2)).then_inc(w_in, 16)
            sp.dma_start(WO[:], wo).then_inc(w_in, 16)
            sp.dma_start(up_weights[:, :, 0:H], w1).then_inc(up_put, 16)
            for c in range(2):
                sp.dma_start(up_weights[:, :, H + c:H + c + 1],
                             b1[:, c * P:(c + 1) * P].rearrange("e (p o) -> e p o", o=1),
                             allow_slow_non_contiguous=True).then_inc(up_put, 16)
            sp.dma_start(X[:, 1, :, :], x_v[1]).then_inc(x_in[1], 16)
            sp.wait_ge(zero_ready, 1)
            for g in range(G):
                for i in range(NT // T):
                    sp.dma_start(rows_in[g][i * P * T:(i + 1) * P * T, :].rearrange("(p t) d -> p (t d)", p=P),
                                 zeros).then_inc(zeroed[g], 16)
                if g == 0:
                    for c in range(2):
                        sp.dma_start(W2[:].rearrange("h (e c o) -> h e c o", e=E, c=2)[:, :, c, :],
                                     w2.rearrange("e (c h) o -> c h e o", c=2)[c]).then_inc(down_in, 16)
                    sp.wait_ge(parts_ready, 1)
                    sp.dma_start(bias2_parts.rearrange("k e h -> e k h"), b2p).then_inc(parts_out, 16)
                    sp.wait_ge(parts_out, 16)
                    sp.dma_start(B2R[:], bias2_parts.rearrange("k e h -> k (e h)")).then_inc(bias_rows, 16)
                if g + 2 < G:
                    sp.dma_start(X[:, g + 2, :, :], x_v[g + 2]).then_inc(x_in[g + 2], 16)
            sp.wait_ge(up_put, up_parts)

            def experts(at, f, g, half, lo, hi):
                slot = SLOT[f, g, half]

                def load_rows(d, old=True):
                    if old:
                        sp.wait_ge(xsT_ps, at - 2 + d * 2)

                def load_weights(d, v, old=True):
                    words = sp.value_load(TE4[0:1, slot, ds(d + lo // 2, 1)], min_val=0, max_val=E ** 4 - 1)
                    for h in range(2):
                        u = 2 * v + h
                        if old:
                            sp.wait_ge(hid_sb, at + (h - 3) + d * 2)
                        for a in range(2):
                            e = (words // E ** (2 * h + a)) % E if 2 * h + a < 3 else words // E ** 3
                            sp.dma_start(WUP[:, u, a, :],
                                         up_weights[ds(e, 1), :, :].rearrange("o d h -> (o d) h")).then_inc(up_in[u], 16)

                def rows(d, v):
                    sp.dma_start(xs[:, v, :, :],
                                 rows_in[slot][ds((d + lo // 2) * 4 * P, 4 * P), :].rearrange("(q p) d -> p q d", p=P)).then_inc(xs_in[v], 16)

                sp.wait_ge(experts_ready, kind_no[("K", f, g, half)] + 1)
                load_weights(0, 0, at > 0)
                which, count = rows_put(f, g, half)
                sp.wait_ge(scattered[which], count)
                for d in range(2):
                    load_rows(d, at > 0)
                    rows(d, d)
                load_weights(1, 1, at > 0)
                if hi - lo > SLOTS:
                    with sp.Fori(1, (hi - lo) // SLOTS) as q:
                        for v in range(2):
                            load_rows(q * 2 + v)
                            rows(q * 2 + v, v)
                            load_weights(q * 2 + v, v)

            waiting = []
            for st in ORDER:
                if st[0] == "E":
                    experts(pairs_at[st], *st[1:])
                    for cn, g in waiting:
                        sp.wait_ge(combined, 4 * (cn + 1))
                        sp.dma_start(out_v[g], X[:, g, :, :]).then_inc(stored, 16)
                    waiting = []
                if st[0] == "C" and st[1] == 1 and st[4] == 4:
                    waiting.append((gathers.index(st[1:3]), st[2]))
            for cn, g in waiting:
                for i in range(4):
                    sp.wait_ge(combined, 4 * cn + i + 1)
                    quarter = slice(i * T // 4, (i + 1) * T // 4)
                    sp.dma_start(out_v[g][:, quarter, :], X[:, g, quarter, :]).then_inc(stored, 16)
            sp.wait_ge(stored, 16 * (G + 3 * len(waiting)))
            for u in range(2):
                sp.wait_ge(eo_out[u], 16 * (pairs // SLOTS))

        @block.gpsimd
        def _(pool):
            chain = [0]

            def link(ins):
                chain[0] += 1
                ins.then_inc(pool_chain, 1)
                pool.wait_ge(pool_chain, chain[0])

            pool.memset(zeros, 0.0).then_inc(zero_ready, 1)
            pool.memset(ones[:], 1.0)
            link(pool.memset(onesf[:], 1.0))
            pool.affine_select(out=ident[:], in_=onesf[:], compare_op=ALU.is_equal, fill=0.0, base=0,
                               pattern=[[-1, P]], channel_multiplier=1)
            pool.affine_select(out=before[:], in_=onesf[:], compare_op=ALU.is_gt, fill=0.0, base=0,
                               pattern=[[1, P]], channel_multiplier=-1)
            link(pool.iota(iota_i[:], [[1, NT]], base=0, channel_multiplier=0))
            link(pool.memset(keep[:], 1.0))
            pool.memset(keep[:, :, 0:1], 0.0)
            pool.tensor_copy(iota_f[:], iota_i[:]).then_inc(consts, 1)

            def scatter(n, f, g, half):
                slot, tiles = SLOT[f, g, half], TILES[f, g, half]
                b, (which, _) = kind_no[("R", f, g)] % XBUF, rows_put(f, g, half)
                pool.wait_ge(rows_ready, n + 1)
                pool.wait_ge(zeroed[slot], 16 * (NT // T))
                for j in range(T - tiles if half else 0, T if half else tiles):
                    for k in range(2):
                        pool.indirect_dma_start(rows_in[slot], bass.IndirectOffsetOnAxis(IDX[:, g, j, k:k + 1], 0),
                                                XL[:, b, j, :], None).then_inc(scattered[which], 16)

            def gather(n, f, g, lo, hi):
                half = lo * T // 4 // TILES[f, g, 0]
                rows = (2 * TILES[f, g, half] + E) * P
                for u in range(2):
                    pool.wait_ge(eo_out[u], 16 * (pairs_by[f, g, half] // SLOTS))
                if n > 0:
                    pool.wait_ge(combined, n * 4)
                for j in range(lo * T // 4, hi * T // 4):
                    for k in range(2):
                        pool.indirect_dma_start(got[:, j, k, :], None, rows_out[SLOT[f, g, half]][0:rows, :],
                                                bass.IndirectOffsetOnAxis(IDX[:, g, j, k:k + 1], 0)).then_inc(got_in[j // 4], 16)

            def normalize(n, g):
                pool.wait_ge(norm_ready, n + 1)
                for j in range(T // 2):
                    ins = pool.tensor_scalar(XN[:, j, :], X[:, g, j, :], rs[:, T + j:T + j + 1], nb[:, T + j:T + j + 1],
                                             mult, add)
                    if j % 4 == 3:
                        ins.then_inc(xn_ready, 1)

            def gate(n):
                pool.wait_ge(proj_act, 20 * (n + 1))
                pool.tensor_tensor(qg[:], qg[:], tmp[3], mult).then_inc(qg_ready, 1)

            for st in ORDER:
                if st[0] == "N" and st[1] is not None and st[2] is not None:
                    normalize(kind_no[st], st[2])
                if st[0] == "A1":
                    gate(kind_no[st])
                if st[0] == "K":
                    scatter(kind_no[st], *st[1:])
                if st[0] == "G":
                    gather(gathers.index(st[1:3]), *st[1:])

        @block.scalar
        def _(act):
            def normalize(normed, g):
                act.wait_ge(norm_ready, normed)
                for j in range(T // 2, T):
                    ins = act.activation(XN[:, j, :], X[:, g, j, :], ACT.Identity,
                                         scale=rs[:, T + j:T + j + 1], bias=nb[:, T + j:T + j + 1])
                    if j % 4 == 3:
                        ins.then_inc(xn_ready_act, 1)

            def route(n):
                for i in range(4):
                    act.wait_ge(xt_ps, 4 * n + i + 1)
                    act.activation(XT[:, i * 512:(i + 1) * 512], ps[i][:], ACT.Copy).then_inc(xt_sb, 1)

            def weigh(n):
                act.wait_ge(gap_ready, n + 1)
                act.activation(gexp[:], gap[:], ACT.Exp).then_inc(gap_exp, 1)

            def experts(at, f, g, half, lo, hi):
                pairs = hi - lo

                def gelu(m, v, u):
                    act.wait_ge(hid_ps, at + m + 1)
                    for k in range(4):
                        ins = act.activation(hidT[:, v, k * P:(k + 1) * P], ps[2 + v][:, k * P:(k + 1) * P], ACT.Gelu,
                                             bias=WUP[:, u, k // 2, H + k % 2:H + k % 2 + 1])
                    ins.then_inc(hid_sb, 1)

                def move_eo(m, u, q=None):
                    act.wait_ge(eo_ps, at + m + 1)
                    if q is not None and u % 2 == 0:
                        act.wait_ge(eo_out[u // 2], 16 * (at // SLOTS + q))
                    act.activation(eo[:, u // 2, u % 2 * 2:u % 2 * 2 + 2, :].rearrange("p a b -> p (a b)"),
                                   ps[6 + u % 2][:, 0:256], ACT.Copy).then_inc(eo_sb, 1)

                def store(m, u):
                    act.wait_ge(eo_sb, at + m + 2)
                    act.dma_start(rows_out[SLOT[f, g, half]][ds((m + lo) * 2 * P, 4 * P), :].rearrange("(q p) d -> p q d", p=P),
                                  eo[:, u // 2, :, :]).then_inc(eo_out[u // 2], 16)

                def move_xsT(m, v):
                    act.wait_ge(xsT_ps, at + m + 1)
                    act.activation(xsT[:, v, :], ps[v][:, 0:256], ACT.Copy).then_inc(xsT_sb, 1)

                def step(m, u, q, static):
                    if not static or m < pairs:
                        gelu(m, u % 2, u)
                    if u % 2 == 1 and (not static or m >= 3):
                        store(m - 3, (u - 3) % SLOTS)
                    if not static or m + 2 < pairs:
                        move_xsT(m + 2, u % 2)
                    if not static or m >= 1:
                        late = q + (u - 1) // SLOTS
                        move_eo(m - 1, (u - 1) % SLOTS, late if not static or late + at > 0 else None)

                move_xsT(0, 0)
                move_xsT(1, 1)
                first = min(pairs, SLOTS if at else 2 * SLOTS)
                for m in range(first):
                    step(m, m % SLOTS, m // SLOTS, True)
                if first < pairs - SLOTS:
                    with act.Fori(first // SLOTS, pairs // SLOTS - 1) as q:
                        for u in range(SLOTS):
                            step(q * SLOTS + u, u, q, False)
                for m in range(max(first, pairs - SLOTS), pairs + 1):
                    step(m, m % SLOTS, m // SLOTS, True)
                store(pairs - 2, (pairs - 2) % SLOTS)

            def turn(n, routed):
                act.wait_ge(logits_ps, routed)
                for i in range(4):
                    act.wait_ge(xnT_ps, 4 * n + i + 1)
                    act.activation(XT[:, i * 512:(i + 1) * 512], ps[i][:], ACT.Copy, scale=GS[:, 0:1]).then_inc(xnT_sb, 1)

            def product(n, k):
                act.wait_ge(proj_ps, 24 * n + k + 1)
                return ps[(6 + k) % 8][:]

            def attention(n):
                for blk in range(4):
                    cols = slice(blk * 512, (blk + 1) * 512)
                    steps = slice(blk * 4, blk * 4 + 4)
                    for w, part in enumerate((cr, ci)):
                        there = product(n, 2 * blk + w)
                        act.activation(part[:, steps, :].rearrange("p a b -> p (a b)"), there, ACT.Copy)
                        act.activation(tmp[w][:, cols], there, ACT.Square).then_inc(proj_act, 1)
                for blk in range(4):
                    there = product(n, 8 + 2 * blk)
                    act.activation(kv[:, blk * 512:(blk + 1) * 512], there, ACT.Copy).then_inc(proj_act, 1)
                act.wait_ge(r2_ready, n + 1)
                act.activation(tmp[2], tmp[0], ACT.Sqrt).then_inc(r_ready, 1)

            def invert(n):
                act.wait_ge(r_ready, n + 1)
                act.activation(tmp[0], tmp[2], ACT.Ln).then_inc(log_ready, 1)
                act.wait_ge(log_ready, n + 1)
                act.activation(tmp[0], tmp[0], ACT.Exp, scale=-1.0).then_inc(inv_ready, 1)

            def gate(n):
                act.activation(tmp[1], tmp[2], ACT.Sigmoid).then_inc(m_ready, 1)
                for blk in range(4):
                    cols = slice(blk * 512, (blk + 1) * 512)
                    act.activation(qg[:, cols], product(n, 16 + 2 * blk), ACT.Copy).then_inc(proj_act, 1)
                    ins = act.activation(tmp[3][:, cols], product(n, 17 + 2 * blk), ACT.Silu)
                    ins.then_inc(proj_act, 1)

            act.wait_ge(w_in, small_weights)
            act.activation(GS[:], GM[:], ACT.Copy, scale=float(D) ** 0.5).then_inc(gs_ready, 1)
            act.wait_ge(gs_ready, 1)
            routed = normed = 0
            for st in ORDER:
                if st[0] == "N":
                    normed += 1
                if st[0] == "R":
                    route(kind_no[st])
                    routed += 1
                if st[0] == "W":
                    weigh(kind_no[st])
                if st[0] == "I":
                    invert(kind_no[st])
                if st[0] == "E":
                    experts(pairs_at[st], *st[1:])
                if st[0] == "T":
                    normalize(normed, st[1])
                    turn(kind_no[st], routed)
                if st[0] == "A":
                    attention(kind_no[st])
                if st[0] == "A1":
                    gate(kind_no[st])

        @block.tensor
        def _(pe):
            def free_banks(st):
                old = psum_before[st]
                if old is None:
                    return
                done = kind_no[old] + 1
                if st[0] == "R":
                    if ranks_by[st] > 0:
                        pe.wait_ge(rank_read, ranks_by[st])
                if old[0] == "E":
                    pe.wait_ge(eo_sb, pairs_at[old] + old[5] - old[4])
                if old[0] == "A":
                    pe.wait_ge(proj_act, 20 * done)
                    pe.wait_ge(proj_dve, 4 * done)
                if old[0] == "A3" and st[0] != "E":
                    pe.wait_ge(x_added, 4 * done)

            def route(st, n):
                free_banks(st)
                if n == 0:
                    pe.wait_ge(consts, 1)
                if n == 0:
                    pe.wait_ge(w_in, small_weights)
                for i in range(5):
                    if i < 4:
                        pe.wait_ge(xl_ready, 4 * n + i + 1)
                        for j in range(4 * i, 4 * i + 4):
                            ins = pe.transpose(ps[i][:, j % 4 * P:(j % 4 + 1) * P], XL[:, n % XBUF, j, :], ident[:])
                        ins.then_inc(xt_ps, 1)
                    if i > 0:
                        pe.wait_ge(xt_sb, 4 * n + i)
                        for j in range(4 * i - 4, 4 * i):
                            ins = pe.matmul(ps[4][:, j * E:(j + 1) * E], XT[:, j * P:(j + 1) * P], WR[:], start=True, stop=True)
                ins.then_inc(logits_ps, 1)

            def rank(n):
                pe.wait_ge(mask_ready, n + 1)
                flat = mask[:].rearrange("p t e -> p (t e)")
                pe.matmul(ps[5][:, 0:T * E], before[:], flat, start=True, stop=True)
                pe.matmul(ps[5][:, T * E:2 * T * E], ones[:], flat, start=True, stop=True).then_inc(rank_ps, 1)

            def experts(st, f, g, half, lo, hi):
                at, pairs, slot = pairs_at[st], hi - lo, SLOT[f, g, half]
                free_banks(st)
                pe.wait_ge(experts_ready, kind_no[("K", f, g, half)] + 1)
                if at == 0:
                    pe.wait_ge(bias_rows, 16)
                    pe.wait_ge(down_in, down_weights)

                def turn_x(m, u, q):
                    if u % 2 == 0:
                        pe.wait_ge(xs_in[u // 2], 16 * (at // SLOTS + q + 1))
                    for a in range(2):
                        ins = pe.transpose(ps[u % 2][:, a * P:(a + 1) * P], xs[:, u // 2, u % 2 * 2 + a, :], ident[:])
                    ins.then_inc(xsT_ps, 1)

                def up(m, u, q):
                    pe.wait_ge(up_in[u], 32 * (at // SLOTS + q + 1))
                    pe.wait_ge(xsT_sb, at + m + 1)
                    for a in range(2):
                        for c in range(2):
                            k = 2 * a + c
                            ins = pe.matmul(ps[2 + u % 2][:, k * P:(k + 1) * P], WUP[:, u, a, c * P:(c + 1) * P],
                                            xsT[:, u % 2, a * P:(a + 1) * P], start=True, stop=True)
                    ins.then_inc(hid_ps, 1)

                def experts_of(m):
                    both = pe.value_load(TE2[0:1, slot, ds(m + lo, 1)], min_val=0, max_val=E * E - 1)
                    return both % E, both // E

                def down(m, v, pair, old, static):
                    pe.wait_ge(hid_sb, at + m + 1)
                    if static and m == 0 and psum_before[st][0] == "A3":
                        pe.wait_ge(x_added, 4 * (kind_no[psum_before[st]] + 1))
                    if old:
                        pe.wait_ge(eo_sb, at + m - 1)
                    for a, e in enumerate(pair):
                        o = ps[6 + v][:, a * D:(a + 1) * D]
                        for c in range(2):
                            pe.matmul(o, hidT[:, v, (2 * a + c) * P:(2 * a + c + 1) * P],
                                      W2[:, ds(e * H + c * D, D)], start=(c == 0), stop=False)
                        ins = pe.matmul(o, ones[0:3, :], B2R[:, ds(e * D, D)], start=False, stop=True)
                    ins.then_inc(eo_ps, 1)

                def step(m, u, q, static):
                    if not static or m < pairs:
                        up(m, u, q)
                    if not static or m >= 1:
                        pair = experts_of(m - 1)
                    if not static or m + 2 < pairs:
                        turn_x(m + 2, (u + 2) % SLOTS, q + (u + 2) // SLOTS)
                    if not static or m >= 1:
                        down(m - 1, (u - 1) % 2, pair, not static or m >= 3, static)

                turn_x(0, 0, 0)
                turn_x(1, 1, 0)
                for m in range(SLOTS):
                    step(m, m, 0, True)
                if pairs > 2 * SLOTS:
                    with pe.Fori(1, pairs // SLOTS - 1) as q:
                        for u in range(SLOTS):
                            step(q * SLOTS + u, u, q, False)
                for m in range(max(SLOTS, pairs - SLOTS), pairs + 1):
                    step(m, m % SLOTS, m // SLOTS, True)

            def turn(st, n):
                free_banks(st)
                for i in range(4):
                    if i < 2:
                        pe.wait_ge(xn_ready, 2 * n + i + 1)
                    else:
                        pe.wait_ge(xn_ready_act, 2 * n + i - 1)
                    for j in range(4):
                        ins = pe.transpose(ps[i][:, j * P:(j + 1) * P], XN[:, 4 * i + j, :], ident[:])
                    ins.then_inc(xnT_ps, 1)

            def attention(n, routed, ranked, some):
                products = [(w, blk) for ws in ((4, 5), (2, 3), (0, 1)) for blk in range(4) for w in ws]
                for k in some:
                    w, blk = products[k]
                    if k == 6:
                        pe.wait_ge(logits_read, routed)
                    if k < 8 and w == 4:
                        pe.wait_ge(xnT_sb, 4 * n + blk + 1)
                    if 2 <= k < 6:
                        pe.wait_ge(xnT_sb, 4 * n + k - 1)
                    if k == 7:
                        pe.wait_ge(rank_read, ranked)
                    if k >= 8:
                        old, old_blk = products[k - 8]
                        if old in (2, 3):
                            pe.wait_ge(proj_dve, 4 * n + old_blk + 1)
                        else:
                            pe.wait_ge(proj_act, 20 * n + k - 7)
                    pe.matmul(ps[(6 + k) % 8][:], WA[:, w, :], XT[:, blk * 512:(blk + 1) * 512],
                              start=True, stop=True).then_inc(proj_ps, 1)

            def project(st, n, g):
                free_banks(st)
                pe.wait_ge(y_ready, n + 1)
                for i in range(4):
                    for j in range(4):
                        ins = pe.matmul(ps[4 + i][:, j * D:(j + 1) * D], kv[:, (4 * i + j) * P:(4 * i + j + 1) * P], WO[:],
                                        start=True, stop=True)
                    ins.then_inc(wo_ps, 1)

            routed = 0
            for st in ORDER:
                if st[0] == "R":
                    route(st, kind_no[st])
                    routed += 1
                if st[0] == "K" and st[3] == 0:
                    rank(kind_no[("R",) + st[1:3]])
                if st[0] == "E":
                    experts(st, *st[1:])
                if st[0] == "T":
                    turn(st, kind_no[st])
                if st[0] == "A0":
                    attention(kind_no[st], routed, ranks_by[st], range(2))
                if st[0] == "A":
                    attention(kind_no[st], routed, ranks_by[st], range(2, 24))
                if st[0] == "A3":
                    project(st, kind_no[st], st[1])

        @block.vector
        def _(dve):
            chain = [0]

            def link(ins, times=1):
                chain[0] += times
                ins.then_inc(dve_chain, 1)
                dve.wait_ge(dve_chain, chain[0])

            def measure(g, col):
                for j in range(T):
                    ins = dve.bn_stats(stats[:, col + j, :], X[:, g, j, :])
                link(ins)

            def norm(n, router, ga):
                if router is not None and router[0] == 0:
                    dve.wait_ge(x_in[router[1]], 16)
                if router is not None:
                    measure(router[1], 0)
                c = slice(0 if router else T, T if ga is None else 2 * T)
                dve.tensor_tensor(df[:, c], stats[:, c, 1], stats[:, c, 4], sub)
                dve.tensor_tensor(var[:, c], stats[:, c, 2], stats[:, c, 5], add)
                link(dve.tensor_tensor(m2[:, c], stats[:, c, 1], stats[:, c, 4], add))
                if router is not None:
                    r = slice(0, T)
                    dve.tensor_scalar(var[:, r], var[:, r], 1.0 / D, EPS, mult, add)
                    ins = dve.scalar_tensor_tensor(out=df[:, r], in0=df[:, r], scalar=0.25, in1=df[:, r], op0=mult, op1=mult)
                if ga is not None:
                    a = slice(T, 2 * T)
                    dve.tensor_scalar(var[:, a], var[:, a], (D + EPS) / D, EPS * EPS, mult, add)
                    ins = dve.scalar_tensor_tensor(out=df[:, a], in0=df[:, a], scalar=0.25 * (D + EPS), in1=df[:, a],
                                                   op0=mult, op1=mult)
                link(ins)
                link(dve.tensor_tensor(var[:, c], var[:, c], df[:, c], add))
                dve.tensor_scalar(vh[:, c], var[:, c], -0.5, None, mult)
                link(dve.tensor_scalar(rs[:, c].bitcast(i32), var[:, c].bitcast(i32), -0.5, float(0x5f3759df), mult, add))
                for _ in range(3):
                    link(dve.tensor_tensor(na[:, c], rs[:, c], rs[:, c], mult))
                    link(dve.tensor_tensor(na[:, c], na[:, c], vh[:, c], mult))
                    link(dve.scalar_tensor_tensor(out=rs[:, c], in0=na[:, c], scalar=1.5, in1=rs[:, c], op0=add, op1=mult))
                dve.scalar_tensor_tensor(out=nb[:, c], in0=m2[:, c], scalar=-0.5, in1=rs[:, c],
                                         op0=mult, op1=mult).then_inc(norm_ready, 1)
                dve.wait_ge(norm_ready, n + 1)
                if router is not None:
                    rn = kind_no[("R",) + router]
                    for st in kind_no:
                        if st[0] == "K" and kind_no[("R",) + st[1:3]] == rn - XBUF:
                            which, count = rows_put(*st[1:])
                            dve.wait_ge(scattered[which], count)
                    normalize(router[1], XL[:, rn % XBUF, :, :], 0, T, xl_ready)
                else:
                    for i in range(G):
                        dve.wait_ge(zeroed[i], 16 * (NT // T))
                    normalize(ga, XN, T, T // 2, xn_ready)

            def normalize(g, out, col, tiles, ready):
                for j in range(tiles):
                    ins = dve.tensor_scalar(out[:, j, :], X[:, g, j, :], rs[:, col + j:col + j + 1], nb[:, col + j:col + j + 1],
                                            mult, add)
                    if j % 4 == 3:
                        ins.then_inc(ready, 1)

            def route(n, f, g):
                xl = XL[:, n % XBUF, :, :]
                dve.wait_ge(xl_ready, (T // 4) * (n + 1))
                xg = X[:, g, :, :].rearrange("p t d -> p (t d)")
                dve.scalar_tensor_tensor(out=xg, in0=xl.rearrange("p t d -> p (t d)"), scalar=0.5, in1=xg, op0=mult, op1=add)
                dve.wait_ge(logits_ps, n + 1)
                dve.tensor_tensor(LG[:], ps[4][:, 0:T * E].rearrange("p (t e) -> p t e", t=T),
                                  BR[:].unsqueeze(1).broadcast_to([P, T, E]), add).then_inc(logits_read, 1)
                dve.wait_ge(logits_read, n + 1)
                for j in range(T):
                    ins = dve.max(MX[:, j, :], LG[:, j, :])
                link(ins)
                dve.tensor_tensor(gap[:], MX[:, :, 1], MX[:, :, 0], sub).then_inc(gap_ready, 1)
                for j in range(T):
                    ins = dve.max_index(IX[:, j, :], MX[:, j, :], LG[:, j, :])
                link(ins)
                link(dve.tensor_copy(IXF[:], IX[:, :, 0:2]))
                for k in range(2):
                    ins = dve.tensor_tensor(hot[:, k, :, :], iota_f[:, 0:E].unsqueeze(1).broadcast_to([P, T, E]),
                                            IXF[:, :, k:k + 1].broadcast_to([P, T, E]), ALU.is_equal)
                link(ins)
                dve.tensor_tensor(mask[:], hot[:, 0, :, :], hot[:, 1, :, :], add).then_inc(mask_ready, 1)

            def rank(n, f, g, half):
                slot, tiles = SLOT[f, g, half], TILES[f, g, half]
                mine = slice(T - tiles if half else 0, T if half else tiles)
                link(dve.memset(cnt[:] if tiles < T else cnt[:, :, 0:1], 0.0))
                dve.wait_ge(rank_ps, kind_no[("R", f, g)] + 1)
                counts = ps[5][:, T * E:2 * T * E].rearrange("p (t e) -> p e t", t=T)
                link(dve.tensor_copy(cnt[:, :, 1 + mine.start:1 + mine.stop], counts[:, :, mine]))
                link(dve.tensor_tensor_scan(off[:].rearrange("p e t -> p (e t)"), keep[:].rearrange("p e t -> p (e t)"),
                                            cnt[:].rearrange("p e t -> p (e t)"), 0.0, mult, add))
                link(dve.tensor_scalar(nte[:], off[:, :, T:T + 1].rearrange("p e o -> p (e o)"), 1.0 / P, 127.0 / 256.0, mult, add))
                link(dve.tensor_scalar(nte[:], nte[:], 12582912.0, -12582912.0, add, add))
                link(dve.tensor_tensor_scan(cum[:], onesf[:, 0:E], nte[:], 0.0, mult, add))
                link(dve.tensor_tensor(basee[:], cum[:], nte[:], sub))
                link(dve.scalar_tensor_tensor(out=off[:, :, 0:T], in0=basee[:].unsqueeze(2).broadcast_to([P, E, T]),
                                              scalar=float(P), in1=off[:, :, 0:T], op0=mult, op1=add))
                ins = dve.tensor_tensor(pos[:], ps[5][:, 0:T * E].rearrange("p (t e) -> p t e", t=T),
                                        off[:, :, 0:T].rearrange("p e t -> p t e"), add)
                ins.then_inc(rank_read, 1)
                dve.wait_ge(rank_read, n + 1)
                for k in range(2):
                    ins = dve.tensor_tensor(sel[:, k, :, :], hot[:, k, :, :], pos[:], mult)
                link(ins)
                for k in range(2):
                    ins = dve.tensor_reduce(rowf[:, :, k:k + 1], sel[:, k, :, :], AX.X, add)
                link(ins)
                dve.tensor_copy(IDX[:, g, mine, :], rowf[:, mine, :]).then_inc(rows_ready, 1)
                link(dve.tensor_tensor(tcmp, iota_f[0:1, :].unsqueeze(2).broadcast_to([1, NT, E]),
                                       cum[0:1, :].unsqueeze(1).broadcast_to([1, NT, E]), ALU.is_ge))
                link(dve.tensor_reduce(tef[:].unsqueeze(2), tcmp, AX.X, add))
                link(dve.tensor_scalar(tef[:], tef[:], float(E - 1), None, ALU.min))
                tef2, tep2 = tef[:].rearrange("o (i a) -> o i a", a=2), tep[:].rearrange("o (i a) -> o i a", a=2)
                link(dve.scalar_tensor_tensor(out=tep[:], in0=tef2[:, :, 1], scalar=float(E), in1=tef2[:, :, 0],
                                              op0=mult, op1=add))
                dve.tensor_copy(TE2[0:1, slot, :], tep[:])
                dve.scalar_tensor_tensor(out=TE4[0:1, slot, :], in0=tep2[:, :, 1], scalar=float(E * E), in1=tep2[:, :, 0],
                                         op0=mult, op1=add).then_inc(experts_ready, 1)
            def weigh(n, g):
                dve.wait_ge(gap_exp, n + 1)
                link(dve.tensor_scalar(den[:], gexp[:], 1.0, None, add))
                link(dve.reciprocal(den[:], den[:]))
                link(dve.tensor_scalar(WGT[:, g, 0, :], den[:], 0.5, None, mult))
                link(dve.tensor_tensor(WGT[:, g, 1, :], WGT[:, g, 0, :], gexp[:], mult))

            def combine(n, g, lo, hi):
                for q in range(lo, hi):
                    dve.wait_ge(got_in[q], 16 * 8 * (n + 1))
                    for k in range(2):
                        for j in range(4 * q, 4 * q + 4):
                            ins = dve.scalar_tensor_tensor(out=X[:, g, j, :], in0=got[:, j, k, :], scalar=WGT[:, g, k, j:j + 1],
                                                           in1=X[:, g, j, :], op0=mult, op1=add)
                        if k == 0:
                            link(ins)
                    ins.then_inc(combined, 1)
                dve.wait_ge(combined, 4 * n + hi)

            def attention(n, g):
                dve.wait_ge(proj_act, 20 * n + 8)
                dve.scalar_tensor_tensor(out=tmp[0], in0=tmp[0], scalar=TINY * TINY, in1=tmp[1],
                                         op0=add, op1=add).then_inc(r2_ready, 1)
                for blk in range(4):
                    cols = slice(blk * 512, (blk + 1) * 512)
                    dve.wait_ge(proj_act, 20 * n + 8 + blk + 1)
                    dve.wait_ge(proj_ps, 24 * n + 8 + 2 * (blk + 1))
                    dve.tensor_tensor(kv[:, cols], ps[(7 + 2 * blk) % 8][:], kv[:, cols], mult).then_inc(proj_dve, 1)

            def gate(n):
                crf, cif = cr[:].rearrange("p l c -> p (l c)"), ci[:].rearrange("p l c -> p (l c)")
                dve.wait_ge(inv_ready, n + 1)
                dve.wait_ge(proj_ps, 24 * (n + 1))
                link(dve.tensor_tensor(XT[:], tmp[2], tmp[0], mult))
                link(dve.scalar_tensor_tensor(out=tmp[0], in0=XT[:], scalar=2.0, in1=tmp[0], op0=sub, op1=mult))
                dve.wait_ge(m_ready, n + 1)
                link(dve.scalar_tensor_tensor(out=tmp[0], in0=tmp[0], scalar=-1.0, in1=tmp[1], op0=mult, op1=mult))
                dve.scalar_tensor_tensor(out=crf, in0=crf, scalar=TINY, in1=tmp[0], op0=add, op1=mult)
                link(dve.tensor_tensor(cif, cif, tmp[0], mult))

            def scan(n):
                k3, q3 = kv[:].rearrange("p (l c) -> p l c", l=T), qg[:].rearrange("p (l c) -> p l c", l=T)
                even, odd = slice(0, T, 2), slice(1, T, 2)
                half = T // 2
                u1, u2 = (XT[:, i * half * P:(i + 1) * half * P].rearrange("p (j c) -> p j c", j=half) for i in range(2))
                for o, x1, x0 in ((span2[:, 2], cr, cr), (u1, ci, ci), (span2[:, 3], cr, ci), (u2, ci, cr),
                                  (span2[:, 0], cr, k3), (span2[:, 1], ci, k3)):
                    ins = dve.tensor_tensor(o, x1[:, odd, :], x0[:, even, :], mult)
                link(ins)
                dve.tensor_tensor(span2[:, 2], span2[:, 2], u1, sub)
                dve.tensor_tensor(span2[:, 3], span2[:, 3], u2, add)
                link(dve.tensor_tensor(span2[:, 0], span2[:, 0], k3[:, odd, :], add))
                for low, high, m in ((span2, span4, 4), (span4, span8, 2), (span8, span16, 1)):
                    for j in range(0, m, 2):
                        w = min(m, 2)
                        p1, p2 = (XT[:, i:i + 4 * w * P].rearrange("p (f j c) -> p f j c", f=4, j=w)
                                  for i in ((0, 1024) if w == 2 else (512, 1024)))
                        first, second = slice(2 * j, 2 * (j + w), 2), slice(2 * j + 1, 2 * (j + w), 2)
                        for p, f in ((p1, 2), (p2, 3)):
                            ins = dve.tensor_tensor(p, low[:, f:f + 1, second, :].broadcast_to([P, 4, w, P]),
                                                    low[:, :, first, :], mult)
                        link(ins)
                        dve.tensor_tensor(high[:, 0:4:2, j:j + w, :], p1[:, 0:4:2], p2[:, 1:4:2], sub)
                        ins = dve.tensor_tensor(high[:, 1:4:2, j:j + w, :], p1[:, 1:4:2], p2[:, 0:4:2], add)
                        link(ins)
                    link(dve.tensor_tensor(high[:, 0:2], high[:, 0:2], low[:, 0:2, 1:2 * m:2, :], add))
                for d, rows in ((1, 4), (2, 4), (4, 4), (8, 2), (4, 2), (2, 2), (1, 2)):
                    first = 2 * d - 1 if rows == 4 or 2 * d == C else 3 * d - 1
                    to, at = slice(first, C, 2 * d), slice(first - d, C - d, 2 * d)
                    m = len(range(first, C, 2 * d))
                    p1, p2 = (XT[:, i:i + rows * BG * m].rearrange("p (f b c) -> p f b c", f=rows, b=BG)
                              for i in (512, 1024))
                    for p, f in ((p1, 2), (p2, 3)):
                        ins = dve.tensor_tensor(p, Y[:, f:f + 1, :, to].broadcast_to([P, rows, BG, m]),
                                                Y[:, 0:rows, :, at], mult)
                    link(ins)
                    link(dve.tensor_tensor(p1[:, 0:2], p1[:, 0:2], Y[:, 0:2, :, to], add))
                    dve.tensor_tensor(Y[:, 0:rows:2, :, to], p1[:, 0:rows:2], p2[:, 1:rows:2], sub)
                    link(dve.tensor_tensor(Y[:, 1:rows:2, :, to], p1[:, 1:rows:2], p2[:, 0:rows:2], add))
                dve.wait_ge(qg_ready, n + 1)
                start = before2[:, :, 0, :].rearrange("p f (b c) -> p f b c", b=BG)
                dve.memset(start[:, :, :, 0:1], 0.0)
                link(dve.tensor_copy(start[:, :, :, 1:C], Y[:, 0:2, :, 0:C - 1]))
                for low, m in ((span8, 1), (span4, 2), (span2, 4)):
                    gap_ = half // m
                    at, to = slice(0, half, gap_), slice(gap_ // 2, half, gap_)
                    p1 = XT[:, 512:512 + 2 * m * P].rearrange("p (f j c) -> p f j c", f=2, j=m)
                    p2 = scratch[:, 0:1024] if m == 4 else XT[:, 1024:1024 + 2 * m * P]
                    p2 = p2.rearrange("p (f j c) -> p f j c", f=2, j=m)
                    for p, f in ((p1, 2), (p2, 3)):
                        ins = dve.tensor_tensor(p, low[:, f:f + 1, 0:2 * m:2, :].broadcast_to([P, 2, m, P]),
                                                before2[:, :, at, :], mult)
                    link(ins)
                    dve.tensor_tensor(before2[:, 0, to, :], p1[:, 0], p2[:, 1], sub)
                    link(dve.tensor_tensor(before2[:, 1, to, :], p1[:, 1], p2[:, 0], add))
                    link(dve.tensor_tensor(before2[:, :, to, :], before2[:, :, to, :], low[:, 0:2, 0:2 * m:2, :], add))
                h, ai_h = span2[:, 0], span2[:, 1]
                dve.tensor_tensor(h, cr[:, even, :], before2[:, 0], mult)
                link(dve.tensor_tensor(ai_h, ci[:, even, :], before2[:, 1], mult))
                link(dve.tensor_tensor(h, h, ai_h, sub))
                link(dve.tensor_tensor(h, h, k3[:, even, :], add))
                dve.tensor_tensor(k3[:, 1:T - 1:2, :], before2[:, 0, 1:half, :], q3[:, 1:T - 1:2, :], mult)
                dve.tensor_tensor(k3[:, T - 1, :], span16[:, 0, 0, :], q3[:, T - 1, :], mult)
                dve.tensor_tensor(k3[:, even, :], h, q3[:, even, :], mult).then_inc(y_ready, 1)

            def add_attention(n, g):
                for i in range(4):
                    dve.wait_ge(wo_ps, 4 * n + i + 1)
                    xq = X[:, g, 4 * i:4 * i + 4, :].rearrange("p t d -> p (t d)")
                    dve.tensor_tensor(xq, ps[4 + i][:], xq, add).then_inc(x_added, 1)
                dve.wait_ge(x_added, 4 * (n + 1))

            dve.wait_ge(bias_in, 16)
            for k in range(2):
                link(dve.tensor_copy(b2p[:, k, :], b2f))
                link(dve.tensor_tensor(b2f, b2f, b2p[:, k, :], sub))
            dve.tensor_copy(b2p[:, 2, :], b2f).then_inc(parts_ready, 1)
            dve.wait_ge(consts, 1)
            dve.wait_ge(w_in, small_weights)
            for st in ORDER:
                if st[0] == "S":
                    measure(st[1], T)
                if st[0] == "N":
                    norm(kind_no[st], st[1], st[2])
                if st[0] == "R":
                    route(kind_no[st], st[1], st[2])
                if st[0] == "K":
                    rank(kind_no[st], *st[1:])
                if st[0] == "W":
                    weigh(kind_no[st], st[2])
                if st[0] == "C":
                    combine(gathers.index(st[1:3]), *st[2:])
                if st[0] == "A":
                    attention(kind_no[st], st[1])
                if st[0] == "A1":
                    gate(kind_no[st])
                if st[0] == "A2":
                    scan(kind_no[st])
                if st[0] == "A3":
                    add_attention(kind_no[st], st[1])


_INS = ["L0_attn_x", "L0_attn_gamma", "L0_attn_wq", "L0_attn_wk", "L0_attn_wv", "L0_attn_wa", "L0_attn_wg", "L0_attn_wo",
        "L0_ffn_Wr", "L0_ffn_br", "L0_ffn_W1", "L0_ffn_b1", "L0_ffn_W2", "L0_ffn_b2"]


def kernel(**inputs):
    import numpy as np
    import concourse.bacc as bacc
    from concourse.bass_utils import run_bass_kernel_spmd as run

    nc = bacc.Bacc("TRN2", target_bir_lowering=False, num_devices=1)
    arrays, args = {}, []
    for name in _INS:
        a = np.ascontiguousarray(inputs[name])
        arrays["in_" + name] = a
        args.append(nc.dram_tensor("in_" + name, a.shape, mybir.dt.from_np(a.dtype), kind="ExternalInput").ap())
    args.append(nc.dram_tensor("out_0", (B, N, D), mybir.dt.float32, kind="ExternalOutput").ap())
    build(nc, *args)
    return run(nc, [arrays], core_ids=[0]).results[0]["out_0"]
```
